# Optimizing a Trainium2 kernel written in Bass

```python
import numpy as np
import jax
import jax.numpy as jnp

def _softmax(x, axis=-1):
    return jax.nn.softmax(x, axis=axis)

def _gelu(x):
    return jax.nn.gelu(x, approximate=True)

def _silu(x):
    return jax.nn.silu(x)

def _sigmoid(x):
    return jax.nn.sigmoid(x)

def _layernorm(x, axis=-1, eps=1e-05):
    m = jnp.mean(x, axis=axis, keepdims=True)
    v = jnp.var(x, axis=axis, keepdims=True)
    return (x - m) / jnp.sqrt(v + eps)

def _scatter_add(tgt, idx, src, axis=0):
    return tgt.at[idx].add(src)

def _segment_sum(src, seg, n):
    return jax.ops.segment_sum(src, seg, n)
kernel_name = 'mk_metaformer_d2_conv_nhwc256_r4_02ba76'

def setup_inputs(seed: int=0):
    np.random.seed(seed)
    _w = jnp.asarray

    def _rec_inputs():
        import jax
        import jax.numpy as jnp
        _gk = jax.random.key(seed)
        x = 7.22e-05 + 1 * jax.random.normal(jax.random.fold_in(_gk, 1), (16, 16, 8, 64), jnp.float32)
        return x
    x = _rec_inputs()

    def _L0_conv_setup():
        import jax, jax.numpy as jnp
        import numpy as np
        E = 2
        EPS = 1e-05

        def _linear_scan(inp, lam):

            def comb(l, r):
                al, bl = l
                ar, br = r
                return (ar * al, ar * bl + br)
            _, h = jax.lax.associative_scan(comb, (lam, inp), axis=0)
            return h

        def _bidir_scan(inp, lam):
            fwd = _linear_scan(inp, lam)
            rev = jnp.flip(_linear_scan(jnp.flip(inp, 0), jnp.flip(lam, 0)), 0)
            return fwd + rev
        key = jax.random.key(seed)
        ks = jax.random.split(key, 7)
        H, W, B, D = (16, 16, 8, 64)
        s = 0.02
        return {'x': jax.random.normal(ks[0], (H, W, B, D), dtype=jnp.float32), 'in_w': jax.random.normal(ks[1], (D, 3 * D), dtype=jnp.float32) * s, 'in_b': jnp.zeros((3 * D,), dtype=jnp.float32), 'out_w': jax.random.normal(ks[2], (D, D), dtype=jnp.float32) * s, 'out_b': jnp.zeros((D,), dtype=jnp.float32), 'gamma': jnp.ones((D,), dtype=jnp.float32), 'beta': jnp.zeros((D,), dtype=jnp.float32)}
    _L0_conv_all = _L0_conv_setup()
    _L0_conv_in = {k: v for k, v in _L0_conv_all.items() if k in ('in_w', 'in_b', 'out_w', 'out_b', 'gamma', 'beta')}
    del _L0_conv_all

    def _L0_ffn_setup():
        import jax, jax.numpy as jnp
        import numpy as np
        D_MODEL = 64
        N_EXPERTS = 16
        HIDDEN = 128
        SCALE = 0.02
        key = jax.random.key(seed)
        ks = jax.random.split(key, 5)
        x = jax.random.normal(ks[0], (4, 2048, D_MODEL), dtype=jnp.float32)
        gate_w = jax.random.normal(ks[1], (D_MODEL, N_EXPERTS), dtype=jnp.float32) * SCALE
        gate_b = jnp.zeros((N_EXPERTS,), dtype=jnp.float32)
        w1 = jax.random.normal(ks[2], (N_EXPERTS, D_MODEL, HIDDEN), dtype=jnp.float32) * SCALE
        w2 = jax.random.normal(ks[3], (N_EXPERTS, D_MODEL, HIDDEN), dtype=jnp.float32) * SCALE
        w3 = jax.random.normal(ks[4], (N_EXPERTS, HIDDEN, D_MODEL), dtype=jnp.float32) * SCALE
        return {'x': x, 'gate_w': gate_w, 'gate_b': gate_b, 'w1': w1, 'w2': w2, 'w3': w3}
    _L0_ffn_all = _L0_ffn_setup()
    _L0_ffn_in = {k: v for k, v in _L0_ffn_all.items() if k in ('gate_w', 'gate_b', 'w1', 'w2', 'w3')}
    del _L0_ffn_all

    def _L1_conv_setup():
        import jax, jax.numpy as jnp
        import numpy as np
        E = 2
        EPS = 1e-05

        def _linear_scan(inp, lam):

            def comb(l, r):
                al, bl = l
                ar, br = r
                return (ar * al, ar * bl + br)
            _, h = jax.lax.associative_scan(comb, (lam, inp), axis=0)
            return h

        def _bidir_scan(inp, lam):
            fwd = _linear_scan(inp, lam)
            rev = jnp.flip(_linear_scan(jnp.flip(inp, 0), jnp.flip(lam, 0)), 0)
            return fwd + rev
        key = jax.random.key(seed)
        ks = jax.random.split(key, 7)
        H, W, B, D = (16, 16, 8, 64)
        s = 0.02
        return {'x': jax.random.normal(ks[0], (H, W, B, D), dtype=jnp.float32), 'in_w': jax.random.normal(ks[1], (D, 3 * D), dtype=jnp.float32) * s, 'in_b': jnp.zeros((3 * D,), dtype=jnp.float32), 'out_w': jax.random.normal(ks[2], (D, D), dtype=jnp.float32) * s, 'out_b': jnp.zeros((D,), dtype=jnp.float32), 'gamma': jnp.ones((D,), dtype=jnp.float32), 'beta': jnp.zeros((D,), dtype=jnp.float32)}
    _L1_conv_all = _L1_conv_setup()
    _L1_conv_in = {k: v for k, v in _L1_conv_all.items() if k in ('in_w', 'in_b', 'out_w', 'out_b', 'gamma', 'beta')}
    del _L1_conv_all

    def _L1_ffn_setup():
        import jax, jax.numpy as jnp
        import numpy as np
        TOP_K = 2
        key = jax.random.key(seed)
        ks = jax.random.split(key, 4)
        B, L, D, H, E = (8, 1024, 64, 256, 8)
        s = 0.02
        return {'x': jax.random.normal(ks[0], (B, L, D), jnp.float32), 'Wg': jax.random.normal(ks[1], (D, E), jnp.float32) * s, 'bg': jnp.zeros((E,), jnp.float32), 'W1': jax.random.normal(ks[2], (E, D, H), jnp.float32) * s, 'b1': jnp.zeros((E, H), jnp.float32), 'W2': jax.random.normal(ks[3], (E, H, D), jnp.float32) * s, 'b2': jnp.zeros((E, D), jnp.float32)}
    _L1_ffn_all = _L1_ffn_setup()
    _L1_ffn_in = {k: v for k, v in _L1_ffn_all.items() if k in ('Wg', 'bg', 'W1', 'b1', 'W2', 'b2')}
    del _L1_ffn_all
    return {'x': x, 'L0_conv_in_w': _L0_conv_in['in_w'], 'L0_conv_in_b': _L0_conv_in['in_b'], 'L0_conv_out_w': _L0_conv_in['out_w'], 'L0_conv_out_b': _L0_conv_in['out_b'], 'L0_conv_gamma': _L0_conv_in['gamma'], 'L0_conv_beta': _L0_conv_in['beta'], 'L0_ffn_gate_w': _L0_ffn_in['gate_w'], 'L0_ffn_gate_b': _L0_ffn_in['gate_b'], 'L0_ffn_w1': _L0_ffn_in['w1'], 'L0_ffn_w2': _L0_ffn_in['w2'], 'L0_ffn_w3': _L0_ffn_in['w3'], 'L1_conv_in_w': _L1_conv_in['in_w'], 'L1_conv_in_b': _L1_conv_in['in_b'], 'L1_conv_out_w': _L1_conv_in['out_w'], 'L1_conv_out_b': _L1_conv_in['out_b'], 'L1_conv_gamma': _L1_conv_in['gamma'], 'L1_conv_beta': _L1_conv_in['beta'], 'L1_ffn_Wg': _L1_ffn_in['Wg'], 'L1_ffn_bg': _L1_ffn_in['bg'], 'L1_ffn_W1': _L1_ffn_in['W1'], 'L1_ffn_b1': _L1_ffn_in['b1'], 'L1_ffn_W2': _L1_ffn_in['W2'], 'L1_ffn_b2': _L1_ffn_in['b2']}

def reference(x, L0_conv_in_w, L0_conv_in_b, L0_conv_out_w, L0_conv_out_b, L0_conv_gamma, L0_conv_beta, L0_ffn_gate_w, L0_ffn_gate_b, L0_ffn_w1, L0_ffn_w2, L0_ffn_w3, L1_conv_in_w, L1_conv_in_b, L1_conv_out_w, L1_conv_out_b, L1_conv_gamma, L1_conv_beta, L1_ffn_Wg, L1_ffn_bg, L1_ffn_W1, L1_ffn_b1, L1_ffn_W2, L1_ffn_b2):
    import jax
    import jax.numpy as jnp

    def _L0_conv_ref(x, in_w, in_b, out_w, out_b, gamma, beta):
        import jax, jax.numpy as jnp
        import numpy as np
        E = 2
        EPS = 1e-05

        def _linear_scan(inp, lam):

            def comb(l, r):
                al, bl = l
                ar, br = r
                return (ar * al, ar * bl + br)
            _, h = jax.lax.associative_scan(comb, (lam, inp), axis=0)
            return h

        def _bidir_scan(inp, lam):
            fwd = _linear_scan(inp, lam)
            rev = jnp.flip(_linear_scan(jnp.flip(inp, 0), jnp.flip(lam, 0)), 0)
            return fwd + rev
        H, W, B, D = x.shape
        nh = D // E
        feat = x @ in_w + in_b
        inp, og, fg = jnp.split(feat, 3, axis=-1)
        inp = jax.nn.silu(inp)
        og = jax.nn.sigmoid(og)
        lam = jax.nn.sigmoid(fg)
        lam = lam.reshape(H, W, B, nh, E)
        inp = inp.reshape(H, W, B, nh, E)
        og = og.reshape(H, W, B, nh, E)
        inp_o = jnp.einsum('...hd,...he->...hde', 1.0 - lam, inp)
        lam_o = jnp.broadcast_to(lam[..., None], inp_o.shape)
        C = nh * E * E
        inp_f = inp_o.reshape(H, W, B, C)
        lam_f = lam_o.reshape(H, W, B, C)
        s_h = _bidir_scan(inp_f, lam_f)
        inp_w = jnp.swapaxes(inp_f, 0, 1)
        lam_w = jnp.swapaxes(lam_f, 0, 1)
        s_w = jnp.swapaxes(_bidir_scan(inp_w, lam_w), 0, 1)
        state = (s_h + s_w).reshape(H, W, B, nh, E, E)
        out = jnp.einsum('...hde,...hd->...he', state, og)
        out = out.reshape(H, W, B, D)
        mu = out.mean(-1, keepdims=True)
        var = out.var(-1, keepdims=True)
        out = (out - mu) * jax.lax.rsqrt(var + EPS) * gamma + beta
        return out @ out_w + out_b

    def _L0_ffn_ref(x, gate_w, gate_b, w1, w2, w3):
        import jax, jax.numpy as jnp
        import numpy as np
        D_MODEL = 64
        N_EXPERTS = 16
        HIDDEN = 128
        SCALE = 0.02
        n_experts = w1.shape[0]
        logits = jnp.einsum('bsd,de->bse', x, gate_w) + gate_b
        probs = jax.nn.softmax(logits, axis=-1)
        top_probs, top_idx = jax.lax.top_k(probs, 2)
        top_probs = top_probs / jnp.sum(top_probs, axis=-1, keepdims=True)
        dispatch = jnp.sum(jax.nn.one_hot(top_idx, n_experts, dtype=x.dtype) * top_probs[..., None], axis=-2)
        h1 = jnp.einsum('bsd,edh->bseh', x, w1)
        h2 = jnp.einsum('bsd,edh->bseh', x, w2)
        hidden = jax.nn.silu(h1) * h2
        expert_out = jnp.einsum('bseh,eho->bseo', hidden, w3)
        return jnp.einsum('bseo,bse->bso', expert_out, dispatch)

    def _L1_conv_ref(x, in_w, in_b, out_w, out_b, gamma, beta):
        import jax, jax.numpy as jnp
        import numpy as np
        E = 2
        EPS = 1e-05

        def _linear_scan(inp, lam):

            def comb(l, r):
                al, bl = l
                ar, br = r
                return (ar * al, ar * bl + br)
            _, h = jax.lax.associative_scan(comb, (lam, inp), axis=0)
            return h

        def _bidir_scan(inp, lam):
            fwd = _linear_scan(inp, lam)
            rev = jnp.flip(_linear_scan(jnp.flip(inp, 0), jnp.flip(lam, 0)), 0)
            return fwd + rev
        H, W, B, D = x.shape
        nh = D // E
        feat = x @ in_w + in_b
        inp, og, fg = jnp.split(feat, 3, axis=-1)
        inp = jax.nn.silu(inp)
        og = jax.nn.sigmoid(og)
        lam = jax.nn.sigmoid(fg)
        lam = lam.reshape(H, W, B, nh, E)
        inp = inp.reshape(H, W, B, nh, E)
        og = og.reshape(H, W, B, nh, E)
        inp_o = jnp.einsum('...hd,...he->...hde', 1.0 - lam, inp)
        lam_o = jnp.broadcast_to(lam[..., None], inp_o.shape)
        C = nh * E * E
        inp_f = inp_o.reshape(H, W, B, C)
        lam_f = lam_o.reshape(H, W, B, C)
        s_h = _bidir_scan(inp_f, lam_f)
        inp_w = jnp.swapaxes(inp_f, 0, 1)
        lam_w = jnp.swapaxes(lam_f, 0, 1)
        s_w = jnp.swapaxes(_bidir_scan(inp_w, lam_w), 0, 1)
        state = (s_h + s_w).reshape(H, W, B, nh, E, E)
        out = jnp.einsum('...hde,...hd->...he', state, og)
        out = out.reshape(H, W, B, D)
        mu = out.mean(-1, keepdims=True)
        var = out.var(-1, keepdims=True)
        out = (out - mu) * jax.lax.rsqrt(var + EPS) * gamma + beta
        return out @ out_w + out_b

    def _L1_ffn_ref(x, Wg, bg, W1, b1, W2, b2):
        import jax, jax.numpy as jnp
        import numpy as np
        TOP_K = 2
        B, L, D = x.shape
        E = W1.shape[0]
        xf = x.reshape(-1, D)
        gate_logits = xf @ Wg + bg
        top_w, top_i = jax.lax.top_k(gate_logits, TOP_K)
        top_w = jax.nn.softmax(top_w, axis=-1)
        w_dense = jnp.sum(jax.nn.one_hot(top_i, E, dtype=xf.dtype) * top_w[..., None], axis=1)
        out = jnp.zeros_like(xf)
        for e in range(E):
            h = jax.nn.gelu(xf @ W1[e] + b1[e], approximate=False)
            out = out + w_dense[:, e:e + 1] * (h @ W2[e] + b2[e])
        return out.reshape(B, L, D)

    def _gn(v, G=32, eps=1e-05):
        B_, H_, W_, C_ = v.shape
        g = v.reshape(B_, H_, W_, G, C_ // G)
        m = jnp.mean(g, axis=(1, 2, 4), keepdims=True)
        s = jnp.var(g, axis=(1, 2, 4), keepdims=True)
        return ((g - m) / jnp.sqrt(s + eps)).reshape(v.shape)

    def _ln_c(v, eps=1e-06):
        m = jnp.mean(v, axis=-1, keepdims=True)
        s = jnp.var(v, axis=-1, keepdims=True)
        return (v - m) / jnp.sqrt(s + eps)

    def _ln_t(v, eps=1e-05):
        m = jnp.mean(v, axis=-1, keepdims=True)
        s = jnp.var(v, axis=-1, keepdims=True)
        return (v - m) / jnp.sqrt(s + eps)

    def _to_tokens(v):
        B_, H_, W_, C_ = v.shape
        return v.reshape(B_, H_ * W_, C_)

    def _from_tokens(t, like):
        return t.reshape(like.shape)
    x = x + _L0_conv_ref(_ln_c(x), L0_conv_in_w, L0_conv_in_b, L0_conv_out_w, L0_conv_out_b, L0_conv_gamma, L0_conv_beta)
    t = _to_tokens(x)
    t = t + _L0_ffn_ref(_ln_t(t), L0_ffn_gate_w, L0_ffn_gate_b, L0_ffn_w1, L0_ffn_w2, L0_ffn_w3)
    x = _from_tokens(t, x)
    x = x + _L1_conv_ref(_ln_c(x), L1_conv_in_w, L1_conv_in_b, L1_conv_out_w, L1_conv_out_b, L1_conv_gamma, L1_conv_beta)
    t = _to_tokens(x)
    t = t + _L1_ffn_ref(_ln_t(t), L1_ffn_Wg, L1_ffn_bg, L1_ffn_W1, L1_ffn_b1, L1_ffn_W2, L1_ffn_b2)
    x = _from_tokens(t, x)
    return x

_drawn_inputs = setup_inputs


def setup_inputs(seed=0):
    import zlib

    import numpy as np

    out = dict(_drawn_inputs(seed))
    spreads = {'L0_conv_in_b': (0.0, 0.1),
     'L0_conv_out_b': (0.0, 0.1),
     'L0_conv_gamma': (1.0, 0.2),
     'L0_conv_beta': (0.0, 0.397),
     'L0_ffn_gate_b': (0.0, 0.8),
     'L1_conv_in_b': (0.0, 0.1),
     'L1_conv_out_b': (0.0, 0.1),
     'L1_conv_gamma': (1.0, 0.2),
     'L1_conv_beta': (0.0, 0.39),
     'L1_ffn_bg': (0.0, 0.1),
     'L1_ffn_b1': (0.0, 0.669),
     'L1_ffn_b2': (0.0, 0.1)}
    factors = {'L0_ffn_gate_w': 8.0,
     'L0_ffn_w1': 8.0,
     'L0_ffn_w2': 8.0,
     'L0_ffn_w3': 8.0,
     'L1_ffn_W1': 3.194,
     'L1_ffn_W2': 2.697}
    for name, (base, spread) in spreads.items():
        noise = np.random.default_rng([zlib.crc32(name.encode()), seed]).standard_normal(out[name].shape)
        drawn = base * np.exp(spread * noise) if base else spread * noise
        out[name] = jnp.asarray(drawn.astype(out[name].dtype))
    for name, factor in factors.items():
        out[name] = (out[name] * factor).astype(out[name].dtype)
    return out
```

```python
import concourse.bass as bass
from concourse import mybir
from contextlib import ExitStack

H, W, B, D = 16, 16, 8, 64
P = 128
GB = 2
GROUPS = B // GB
LAYERS = 2
UNITS = LAYERS * GROUPS
TOK = GB * H * W
HALF = H * W // P
TILES = GB * HALF
SEQ = 16
NSEQ = TOK // SEQ
PAD = SEQ + 1
SCAN = NSEQ * PAD + 1
EXPERTS = (16, 8)
STEPS = EXPERTS
PAIRS = tuple(e // 2 for e in EXPERTS)
HID = 128
EPS_C = 1e-6
EPS_T = 1e-5
LAG = 3


def layer(u):
    return u // GROUPS


def steps_before(u):
    return sum(STEPS[layer(v)] for v in range(u))


def pairs_before(u):
    return steps_before(u) // 2


def adds_before(u):
    return pairs_before(u) - u


SLOTS = 16
C_STAGES, E_STAGES = 13, 8
BEFORE = C_STAGES + 3
X_FROM = 7


def schedule():
    slots = [(-1, j) for j in range(BEFORE)] + [(u, j) for u in range(UNITS) for j in range(SLOTS)]
    plan, m2_before, m2_last = {}, {}, None
    c, c_stage, c_done, e, e_stage, x, x_stage = 0, 0, 0, 0, 0, 0, 0
    for u, j in slots:
        here = []
        c_was_done, x_was_done = c_done, x
        if c < UNITS and (c < GROUPS or c_stage or x_was_done > c - GROUPS):
            here.append(("C", c, c_stage))
            c_stage += 1
            if c_stage == C_STAGES:
                c, c_stage, c_done = c + 1, 0, c + 1
        x_open = x == u - 1 and j >= X_FROM
        if x_stage or (x_open and not e_stage and (j + E_STAGES >= SLOTS or not (e <= u + 1 and e < c_was_done))):
            if not x_stage:
                m2_before["X", x], m2_last = m2_last, ("X", x)
            here.append(("X", x, x_stage))
            x_stage += 1
            if x_stage == 2:
                x, x_stage = x + 1, 0
        elif e < UNITS and e <= u + 1 and e < c_was_done:
            for _ in range(E_STAGES - e_stage if j == SLOTS - 1 and e == u + 1 else 1):
                if not e_stage:
                    m2_before["E", e], m2_last = m2_last, ("E", e)
                here.append(("E", e, e_stage))
                e_stage += 1
            if e_stage == E_STAGES:
                e, e_stage = e + 1, 0
        plan[u, j] = here
    m2_before["X", UNITS - 1] = m2_last
    assert c == UNITS and e == UNITS and x == UNITS - 1
    return ([plan[-1, j] for j in range(BEFORE)], [[plan[u, j] for j in range(SLOTS)] for u in range(UNITS)],
            m2_before)


def metaformer(nc, x, L0_conv_in_w, L0_conv_in_b, L0_conv_out_w, L0_conv_out_b, L0_conv_gamma, L0_conv_beta,
               L0_ffn_gate_w, L0_ffn_gate_b, L0_ffn_w1, L0_ffn_w2, L0_ffn_w3,
               L1_conv_in_w, L1_conv_in_b, L1_conv_out_w, L1_conv_out_b, L1_conv_gamma, L1_conv_beta,
               L1_ffn_Wg, L1_ffn_bg, L1_ffn_W1, L1_ffn_b1, L1_ffn_W2, L1_ffn_b2, out):
    fp32, fp32r = mybir.dt.float32, mybir.dt.float32r
    i32, u32 = mybir.dt.int32, mybir.dt.uint32
    ALU = mybir.AluOpType
    ACT = mybir.ActivationFunctionType

    conv_in_w, conv_in_b = (L0_conv_in_w, L1_conv_in_w), (L0_conv_in_b, L1_conv_in_b)
    conv_out_w, conv_out_b = (L0_conv_out_w, L1_conv_out_w), (L0_conv_out_b, L1_conv_out_b)
    gamma, beta = (L0_conv_gamma, L1_conv_gamma), (L0_conv_beta, L1_conv_beta)
    gate_w, gate_b = (L0_ffn_gate_w, L1_ffn_Wg), (L0_ffn_gate_b, L1_ffn_bg)
    x_rows = x.rearrange("h w (g i) d -> (h w) g i d", g=GROUPS)
    out_rows = out.rearrange("h w (g i) d -> (h w) g i d", g=GROUPS)

    before, beside, m2_before = schedule()

    ctx = ExitStack()
    with ctx:
        def sb(name, shape, dt=fp32):
            return ctx.enter_context(nc.sbuf_tensor(name, shape, dt))

        def sem(name):
            return ctx.enter_context(nc.semaphore(name))

        ident = sb("ident", [P, P])
        iota_i = sb("iota_i", [P, 16], i32)
        iota = sb("iota", [P, 16])
        minus_half = sb("minus_half", [P, TILES])
        rows = sb("rows", [P, GROUPS, GB, HALF, D])
        in_raw = sb("in_raw", [P, LAYERS, 3 * D])
        in_wide = sb("in_wide", [P, LAYERS, 3, P])
        in_hi = sb("in_hi", [P, LAYERS, 3, P], fp32r)
        in_lo = sb("in_lo", [P, LAYERS, 3, P], fp32r)
        out_raw = sb("out_raw", [P, LAYERS, D])
        out_scaled = sb("out_scaled", [P, LAYERS, D])
        out_hi = sb("out_hi", [P, LAYERS, D], fp32r)
        out_lo = sb("out_lo", [P, LAYERS, D], fp32r)
        gate_raw = sb("gate_raw", [P, LAYERS, 16])
        gate_hi = sb("gate_hi", [P, LAYERS, 16], fp32r)
        gate_lo = sb("gate_lo", [P, LAYERS, 16], fp32r)
        vectors = sb("vectors", [20 + LAYERS * 7, P])
        columns = sb("columns", [P, 20 + LAYERS * 7])
        half_bias = sb("half_bias", [P, LAYERS, 3])
        out_bias = sb("out_bias", [D, LAYERS])
        up_raw = sb("up_raw", [P, 16, 2, HID])
        up_hi0 = sb("up_hi0", [P, 16, 2, HID], fp32r)
        up_lo0 = sb("up_lo0", [P, 16, 2, HID], fp32r)
        up_hi1 = sb("up_hi1", [P, 8, 2, HID], fp32r)
        up_lo1 = sb("up_lo1", [P, 8, 2, HID], fp32r)
        down0 = sb("down0", [P, 16, D])
        down1 = sb("down1", [P, 8, 2, D])
        stats = {n: sb(f"stats_{n}", [P, TILES, 6]) for n in "ce"}
        moments = {n: sb(f"moments_{n}", [P, TILES, 2]) for n in "ce"}
        spread = {n: sb(f"spread_{n}", [P, TILES]) for n in "ce"}
        rstd = {n: sb(f"rstd_{n}", [P, TILES]) for n in "ce"}
        norm = {n: sb(f"norm_{n}", [P, TILES, D]) for n in "ce"}
        parts = {n: sb(f"parts_{n}", [P, TILES, 2, D]) for n in "ce"}
        conv_z = sb("conv_z", [P, TOK], fp32r)
        tanh_f = sb("tanh_f", [P, TOK])
        tanh_i = sb("tanh_i", [P, TOK])
        tanh_o = sb("tanh_o", [P, TOK])
        sig_i = sb("sig_i", [P, TOK])
        silu_i = sb("silu_i", [P, TOK])
        lam_w = sb("lam_w", [P, SCAN])
        lam_h = sb("lam_h", [P, SCAN])
        add_w = sb("add_w", [P, SCAN])
        add_h = sb("add_h", [P, SCAN])
        fwd_w, rev_w, fwd_h, rev_h = (sb(n, [P, SCAN]) for n in ("fwd_w", "rev_w", "fwd_h", "rev_h"))
        sum_w = sb("sum_w", [P, TOK])
        sum_h = sb("sum_h", [P, TOK])
        gated = sb("gated", [P, TOK])
        heads = sb("heads", [P, TILES, D])
        conv_y = sb("conv_y", [D, TOK])
        tok_z = sb("tok_z", [P, 2, TOK], fp32r)
        logits_t = sb("logits_t", [16, TOK])
        logits = sb("logits", [P, TILES, 16])
        best = sb("best", [P, TILES, 8])
        best_at = sb("best_at", [P, TILES, 8], u32)
        best_atf = sb("best_atf", [P, TILES, 2])
        margin = sb("margin", [P, TILES])
        tanh_m = sb("tanh_m", [P, TILES])
        shares = sb("shares", [P, TILES, 2])
        pick = sb("pick", [P, 2, TILES, 16])
        gates = sb("gates", [P, TILES, 16])
        gates_t = sb("gates_t", [16, TOK])
        gates_b = sb("gates_b", [P, 2, 8, TOK])
        silu_h = sb("silu_h", [P, 2, TOK])
        hidden = sb("hidden", [P, 4, 2, TOK])
        weighted = sb("weighted", [P, 2, TOK])
        total = sb("total", [P, 2, TOK])

        gates_dram = nc.dram_tensor("gates_dram", (UNITS, 16, TOK), fp32, kind="Internal").ap()

        UP = ctx.enter_context(nc.psum_tensor("UP", [P, 4, TOK], fp32))
        DOWN = ctx.enter_context(nc.psum_tensor("DOWN", [P, TOK], fp32))
        M0, M1, M2 = (ctx.enter_context(nc.psum_tensor(n, [P, TOK], fp32)) for n in ("M0", "M1", "M2"))

        F_B, O_B, I_B, GAMMA, BETA, OUT_B, GATE_B = range(7)

        def column(l, which, n=P):
            at = 20 + 7 * l + which
            return columns[0:n, at:at + 1]

        FORGET, INPUT, OUTPUT = range(3)

        def tiles(t):
            return t.rearrange("p (t n) -> p t n", t=TILES)

        def body(t):
            return t[:, 0:NSEQ * PAD].rearrange("p (s n) -> p s n", n=PAD)[:, :, 1:PAD]

        def by_image(ap):
            return ap.rearrange("p (i s) n -> p i s n", i=GB)

        def turned(ap):
            return ap.rearrange("p (i s) n -> p i n s", i=GB)

        def square(t):
            return t.rearrange("p (i s n) -> p i s n", i=GB, s=H)

        s_x = [sem(f"rows_loaded{g}") for g in range(GROUPS)]
        s_small = [sem(f"conv_weights_loaded{l}") for l in range(LAYERS)]
        s_up = [sem(f"up_loaded{p}") for p in range(12)]
        s_down = [sem(f"down_loaded{l}") for l in range(LAYERS)]
        s_vectors = sem("vectors_loaded")
        s_const = sem("constants_ready")
        s_pads = sem("pads_zeroed")
        s_outb = sem("out_bias_product")
        s_outb_ready = sem("out_bias_ready")
        s_conv_w = sem("conv_weights_split")
        s_hi = sem("up_high_parts")
        s_split = sem("up_pairs_split")
        s_vturn = sem("vectors_turned")
        s_columns = sem("columns_ready")
        s_dve = sem("vector_chain")
        s_pool = sem("pool_chain")
        s_stats = {n: sem(f"moments_ready_{n}") for n in "ce"}
        s_rstd = {n: sem(f"rstd_ready_{n}") for n in "ce"}
        s_parts = {n: sem(f"norm_parts_ready_{n}") for n in "ce"}
        s_turn = {n: sem(f"norm_turned_{n}") for n in "ce"}
        s_z = {n: sem(f"norm_columns_ready_{n}") for n in "ce"}
        s_proj = sem("projections_done")
        s_tanh_f = sem("tanh_f_ready")
        s_tanh_i = sem("tanh_i_ready")
        s_tanh_o = sem("tanh_o_ready")
        s_sig = sem("sigmoids_ready")
        s_silu = sem("silu_i_ready")
        s_add_w = sem("row_inputs_ready")
        s_add_h = sem("column_inputs_ready")
        s_scan_w = sem("row_scans_done")
        s_scan_h = sem("column_scans_done")
        s_sum_w = sem("row_scans_summed")
        s_gated = sem("gated_ready")
        s_gturn = sem("gated_turned")
        s_heads = sem("heads_ready")
        s_y = sem("conv_output_product")
        s_yc = sem("conv_output_copied")
        s_yturn = sem("conv_output_turned")
        s_conv = sem("conv_residual_done")
        s_lg = sem("logits_product")
        s_lgc = sem("logits_copied")
        s_lgturn = sem("logits_turned")
        s_margin = sem("margin_ready")
        s_lgread = sem("logits_read")
        s_tm = sem("margin_tanh")
        s_gates = sem("gates_ready")
        s_gateturn = sem("gates_turned")
        s_gatec = sem("gates_copied")
        s_gsent = [sem(f"gates_sent{k}") for k in range(2)]
        s_gback = [sem(f"gates_broadcast{k}") for k in range(2)]
        s_upa = sem("up_first_bank")
        s_upb = sem("up_second_bank")
        s_silu_h = sem("silu_ready")
        s_hid0 = sem("hidden_ready0")
        s_hid1 = sem("hidden_ready1")
        s_dn = sem("pair_down_done")
        s_pm = sem("pair_weighted")
        s_sum = sem("pair_added")
        s_xturn = sem("total_turned")
        s_exit = sem("exit_residual_done")
        s_out = sem("rows_stored")

        N0 = steps_before(GROUPS)

        def wait_hidden(eng, n):
            if n < N0:
                eng.wait_ge(s_hid0, n + 1)
            else:
                eng.wait_ge(s_hid1, n + 1 - N0)

        def each_slot(u):
            per = SLOTS // STEPS[layer(u)]
            for i in range(STEPS[layer(u)]):
                yield i, [s for j in range(per) for s in beside[u][per * i + j]]

        block = ctx.enter_context(nc.Block())

        @block.sync
        def _(sp):
            def load_rows(g):
                for half in range(HALF):
                    sp.dma_start(rows[:, g, :, half, :], x_rows[half * P:(half + 1) * P, g, :, :]).then_inc(s_x[g], 16)

            def load_up(pair):
                for k in range(2):
                    part = slice(k * D, (k + 1) * D)
                    if pair < 8:
                        e = slice(2 * pair, 2 * pair + 2)
                        for n, w in enumerate((L0_ffn_w1, L0_ffn_w2)):
                            sp.dma_start(up_raw[part, e, n, :], w[e, :, :].rearrange("e d h -> d e h")).then_inc(s_up[pair], 16)
                    else:
                        e = slice(2 * pair - 16, 2 * pair - 14)
                        sp.dma_start(up_raw[part, e, :, :],
                                     L1_ffn_W1[e, :, :].rearrange("e d (j h) -> d e j h", j=2)).then_inc(s_up[pair], 16)

            for g in range(2):
                load_rows(g)
            load_up(0)
            load_up(1)
            for g in range(2, GROUPS):
                load_rows(g)
            for pair in range(2, 8):
                load_up(pair)
            sp.dma_start(down0[:, :, :], L0_ffn_w3.rearrange("e h o -> h e o")).then_inc(s_down[0], 16)
            sp.dma_start(down1[:, :, :, :], L1_ffn_W2.rearrange("e (j h) o -> h e j o", j=2)).then_inc(s_down[1], 16)
            sp.wait_ge(s_split, 8)
            for pair in range(8, 12):
                load_up(pair)

            def broadcast_gates(u):
                sp.wait_ge(s_gatec, u + 1)
                e = EXPERTS[layer(u)]
                sp.dma_start(gates_dram[u, 0:e, :], gates_t[0:e, :]).then_inc(s_gsent[u % 2], 16)
                sp.wait_ge(s_gsent[u % 2], 16 * (u // 2 + 1))
                if u >= 2:
                    sp.wait_ge(s_pm, pairs_before(u - 1))
                by_pair = gates_dram[u, 0:e, :].rearrange("(q k) n -> k q n", k=2)
                for k in range(2):
                    sp.dma_start(gates_b[k * D:(k + 1) * D, u % 2, 0:e // 2, :],
                                 by_pair[k:k + 1, :, :].broadcast_to([D, e // 2, TOK])).then_inc(s_gback[u % 2], 16)

            def store_rows(u):
                g = u % GROUPS
                sp.wait_ge(s_exit, u + 1)
                for half in range(HALF):
                    sp.dma_start(out_rows[half * P:(half + 1) * P, g, :, :], rows[:, g, :, half, :]).then_inc(s_out, 16)

            for u in range(UNITS):
                broadcast_gates(u)
                if u >= GROUPS + 2:
                    store_rows(u - 2)
            for u in (UNITS - 2, UNITS - 1):
                store_rows(u)
            sp.wait_ge(s_out, 16 * HALF * GROUPS)

        @block.gpsimd
        def _(pool):
            chain = [0]

            def link(ins):
                chain[0] += 1
                ins.then_inc(s_pool, 1)
                pool.wait_ge(s_pool, chain[0])

            link(nc.gpsimd.memset(ident[:, :], 0.0))
            nc.gpsimd.affine_select(out=ident[:, :], in_=ident[:, :], compare_op=ALU.not_equal, fill=1.0, base=0,
                                    pattern=[[-1, P]], channel_multiplier=1).then_inc(s_const, 1)
            nc.gpsimd.iota(iota_i[:, :], [[1, 16]], base=0, channel_multiplier=0).then_inc(s_const, 1)
            link(nc.gpsimd.memset(minus_half[:, :], -0.5))
            for t in (lam_w, lam_h, add_w, add_h):
                last = nc.gpsimd.memset(t[:, :], 0.0)
            last.then_inc(s_pads, 1)

            def make_rstd(n, count, eps):
                pool.wait_ge(s_stats[n], count)
                link(nc.gpsimd.tensor_scalar(spread[n][:, :], moments[n][:, :, 1], eps, None, ALU.add))
                nc.gpsimd.tensor_tensor(rstd[n][:, :], spread[n][:, :], minus_half[:, :], ALU.pow).then_inc(s_rstd[n], 1)

            def split_up(pair):
                hi, lo = (up_hi0, up_lo0) if pair < 8 else (up_hi1, up_lo1)
                e = slice(2 * pair % 16, 2 * pair % 16 + 2)
                pool.wait_ge(s_hi, pair + 1)
                pool.wait_ge(s_up[pair], 64 if pair < 8 else 32)
                nc.gpsimd.tensor_tensor(lo[:, e, :, :], up_raw[:, e, :, :], hi[:, e, :, :].bitcast(fp32),
                                        ALU.subtract).then_inc(s_split, 1)

            def conv(u, k):
                if k == 0:
                    make_rstd("c", 2 * u + 1, EPS_C)
                elif k == 5:
                    pool.wait_ge(s_scan_w, u + 1)
                    if u:
                        pool.wait_ge(s_gated, u)
                    nc.gpsimd.tensor_tensor(square(sum_w[:, :]), by_image(body(fwd_w)), by_image(body(rev_w)),
                                            ALU.add).then_inc(s_sum_w, 1)
                elif k == 8:
                    make_rstd("c", 2 * u + 2, 4 * EPS_T)

            def entry(u, k):
                if k == 0:
                    make_rstd("e", u + 1, EPS_T)

            def add_pair(u, i):
                q = pairs_before(u) + i
                if i == 0:
                    return
                pool.wait_ge(s_pm, q + 1)
                if i > 1:
                    pool.wait_ge(s_sum, adds_before(u) + i - 1)
                t = total[:, u % 2, :]
                nc.gpsimd.tensor_tensor(t, t, weighted[:, q % 2, :], ALU.add).then_inc(s_sum, 1)

            def stages(slot):
                for part, u, k in slot:
                    if part == "C":
                        conv(u, k)
                    elif part == "E":
                        entry(u, k)

            pair = 0
            for j, slot in enumerate(before):
                stages(slot)
                if j >= 2 and j % 2 == 0 and pair < 8:
                    split_up(pair)
                    pair += 1
            while pair < 8:
                split_up(pair)
                pair += 1
            for u in range(UNITS):
                for i, slot in each_slot(u):
                    if i % 2 == 0:
                        if i >= 4:
                            add_pair(u, i // 2 - 2)
                        elif u:
                            add_pair(u - 1, PAIRS[layer(u - 1)] + i // 2 - 2)
                    stages(slot)
                    if u == 1 and i % 4 == 3:
                        split_up(pair)
                        pair += 1
            for i in (-2, -1):
                add_pair(UNITS - 1, PAIRS[1] + i)

        @block.scalar
        def _(act):
            def load_conv(l):
                s = s_small[l]
                e = EXPERTS[l]
                for k in range(2):
                    part = slice(k * D, (k + 1) * D)
                    act.dma_start(in_raw[part, l, :], conv_in_w[l]).then_inc(s, 16)
                    act.dma_start(out_raw[part, l, :], conv_out_w[l]).then_inc(s, 16)
                    act.dma_start(gate_raw[part, l, 0:e], gate_w[l]).then_inc(s, 16)

            def load_vectors(l):
                def row(which):
                    return vectors[20 + 7 * l + which:21 + 7 * l + which, :]

                for k in range(2):
                    for which, start in ((F_B, 2 * D), (O_B, D)):
                        act.dma_start(row(which).rearrange("a (m e) -> a m e", e=2)[:, :, k:k + 1],
                                      conv_in_b[l][start:start + D].rearrange("(a m e) -> a m e", a=1, e=1),
                                      allow_slow_non_contiguous=True).then_inc(s_vectors, 16)
                    act.dma_start(row(I_B).rearrange("a (h d e) -> a h d e", d=2, e=2)[:, :, k, :],
                                  conv_in_b[l][0:D].rearrange("(a h e) -> a h e", a=1, e=2)).then_inc(s_vectors, 16)
                for which, src in ((GAMMA, gamma[l]), (BETA, beta[l]), (OUT_B, conv_out_b[l]), (GATE_B, gate_b[l])):
                    n = src.shape[0]
                    act.dma_start(row(which).rearrange("a (r n) -> a r n", n=n),
                                  src.rearrange("(a r n) -> a r n", a=1, r=1).broadcast_to([1, P // n, n])
                                  ).then_inc(s_vectors, 16)

            load_vectors(0)
            load_vectors(1)
            act.dma_start(vectors[0:16, :], L1_ffn_b1.rearrange("e (j h) -> (e j) h", j=2)).then_inc(s_vectors, 16)
            act.dma_start(vectors[16:20, :], L1_ffn_b2.rearrange("(q k) o -> q (k o)", k=2)).then_inc(s_vectors, 16)
            for l in range(LAYERS):
                load_conv(l)

            def round_up(pair):
                hi = up_hi0 if pair < 8 else up_hi1
                e = slice(2 * pair % 16, 2 * pair % 16 + 2)
                act.wait_ge(s_up[pair], 64 if pair < 8 else 32)
                nc.scalar.activation(hi[:, e, :, :], up_raw[:, e, :, :], ACT.Copy).then_inc(s_hi, 1)

            def conv(u, k):
                l = layer(u)
                if k in (2, 10):
                    count = 2 * u + (1 if k == 2 else 2)
                    act.wait_ge(s_turn["c"], count)
                    if count > 1:
                        act.wait_ge(s_proj if k == 10 else s_y, 3 * u + 3 if k == 10 else u)
                    nc.scalar.activation(conv_z[:, :], (M0 if k == 2 else M1)[:, :], ACT.Copy).then_inc(s_z["c"], 1)
                elif k == 3:
                    if u:
                        act.wait_ge(s_gated, u)
                        act.wait_ge(s_scan_h, u)
                    else:
                        act.wait_ge(s_conv_w, 1)
                        act.wait_ge(s_pads, 1)
                    act.wait_ge(s_proj, 3 * u + 1)
                    nc.scalar.activation(tanh_f[:, :], M1[:, :], ACT.Tanh, bias=half_bias[:, l, F_B:F_B + 1],
                                         scale=0.5).then_inc(s_tanh_f, 1)
                    act.wait_ge(s_proj, 3 * u + 2)
                    nc.scalar.activation(tanh_i[:, :], M0[:, :], ACT.Tanh, bias=half_bias[:, l, I_B:I_B + 1],
                                         scale=0.5).then_inc(s_tanh_i, 1)
                    act.wait_ge(s_tanh_f, u + 1)
                    nc.scalar.activation(by_image(body(lam_w)), square(tanh_f[:, :]), ACT.Copy, bias=0.5,
                                         scale=0.5)
                    act.wait_ge(s_tanh_i, u + 1)
                    nc.scalar.activation(sig_i[:, :], tanh_i[:, :], ACT.Copy, bias=0.5, scale=0.5).then_inc(s_sig, 1)
                    act.wait_ge(s_proj, 3 * u + 3)
                    nc.scalar.activation(tanh_o[:, :], M1[:, :], ACT.Tanh, bias=half_bias[:, l, O_B:O_B + 1],
                                         scale=0.5).then_inc(s_tanh_o, 1)
                    nc.scalar.activation(turned(body(lam_h)), square(tanh_f[:, :]), ACT.Copy, bias=0.5, scale=0.5)
                elif k == 4:
                    act.wait_ge(s_add_w, u + 1)
                    nc.scalar.activation(turned(body(add_h)), by_image(body(add_w)), ACT.Copy).then_inc(s_add_h, 1)
                elif k == 11:
                    act.wait_ge(s_y, u + 1)
                    if u:
                        act.wait_ge(s_yturn, u)
                    else:
                        act.wait_ge(s_outb_ready, 2)
                    nc.scalar.activation(conv_y[:, :], M0[0:D, :], ACT.Identity,
                                         bias=out_bias[:, l:l + 1]).then_inc(s_yc, 1)

            def entry(u, k):
                l = layer(u)
                e = EXPERTS[l]
                if k == 2:
                    act.wait_ge(s_turn["e"], u + 1)
                    if u >= 2:
                        act.wait_ge(s_upb, steps_before(u - 1))
                    nc.scalar.activation(tok_z[:, u % 2, :], M2[:, :], ACT.Copy).then_inc(s_z["e"], 1)
                elif k == 3:
                    act.wait_ge(s_lg, u + 1)
                    act.wait_ge(s_columns, 1)
                    if u:
                        act.wait_ge(s_lgturn, u)
                    nc.scalar.activation(logits_t[0:e, :], M2[0:e, :], ACT.Identity,
                                         bias=column(l, GATE_B, e)).then_inc(s_lgc, 1)
                elif k == 5:
                    act.wait_ge(s_margin, u + 1)
                    nc.scalar.activation(tanh_m[:, :], margin[:, :], ACT.Tanh, scale=0.5).then_inc(s_tm, 1)
                elif k == 7:
                    act.wait_ge(s_gateturn, u + 1)
                    if u:
                        act.wait_ge(s_gsent[(u - 1) % 2], 16 * ((u - 1) // 2 + 1))
                    nc.scalar.activation(gates_t[0:e, :], M2[0:e, :], ACT.Copy).then_inc(s_gatec, 1)

            def step(u, i):
                n = steps_before(u) + i
                a = 2 * (n % 2)
                act.wait_ge(s_upa, n + 1)
                if layer(u) == 0:
                    if n >= 2:
                        act.wait_ge(s_hid0, n - 1)
                    nc.scalar.activation(silu_h[:, n % 2, :], UP[:, a, :], ACT.Silu).then_inc(s_silu_h, 1)
                else:
                    act.wait_ge(s_dn, (n - 4) // 2 + 1)
                    nc.scalar.activation(hidden[:, n % 4, 0, :], UP[:, a, :], ACT.Gelu,
                                         bias=columns[:, 2 * i:2 * i + 1])
                    act.wait_ge(s_upb, n + 1)
                    nc.scalar.activation(hidden[:, n % 4, 1, :], UP[:, a + 1, :], ACT.Gelu,
                                         bias=columns[:, 2 * i + 1:2 * i + 2]).then_inc(s_hid1, 1)

            def stages(slot):
                for part, u, k in slot:
                    if part == "C":
                        conv(u, k)
                    elif part == "E":
                        entry(u, k)

            pair = 0
            for j, slot in enumerate(before):
                stages(slot)
                if j >= 2 and j % 2 == 0 and pair < 8:
                    round_up(pair)
                    pair += 1
            while pair < 8:
                round_up(pair)
                pair += 1
            for u in range(UNITS):
                for i, slot in each_slot(u):
                    step(u, i)
                    stages(slot)
                    if u == 1 and i % 4 == 3:
                        round_up(pair)
                        pair += 1

        @block.vector
        def _(dve):
            chain = [0]

            def link(ins):
                chain[0] += 1
                ins.then_inc(s_dve, 1)
                dve.wait_ge(s_dve, chain[0])

            def conv_weights(l):
                dve.wait_ge(s_small[l], 16 * 6)
                fog = in_wide[:, l, :, :]
                for e in range(2):
                    nc.vector.tensor_copy(fog[:, FORGET, e:P:2], in_raw[:, l, 2 * D:3 * D])
                    nc.vector.tensor_copy(fog[:, OUTPUT, e:P:2], in_raw[:, l, D:2 * D])
                    d = e
                    last = nc.vector.tensor_copy(
                        fog[:, INPUT, :].rearrange("p (h d e) -> p h d e", d=2, e=2)[:, :, d, :],
                        in_raw[:, l, 0:D].rearrange("p (h e) -> p h e", e=2))
                nc.vector.tensor_scalar(out_scaled[:, l, :], out_raw[:, l, :], column(l, GAMMA), -1.0,
                                        ALU.mult, ALU.mult)
                link(nc.vector.tensor_scalar(half_bias[:, l, :], columns[:, 20 + 7 * l:23 + 7 * l], 0.5, None, ALU.mult))
                e = EXPERTS[l]
                nc.vector.tensor_copy(in_hi[:, l, :, :], fog)
                nc.vector.tensor_copy(out_hi[:, l, :], out_scaled[:, l, :])
                link(nc.vector.tensor_copy(gate_hi[:, l, 0:e], gate_raw[:, l, 0:e]))
                nc.vector.tensor_tensor(in_lo[:, l, :, :], fog, in_hi[:, l, :, :].bitcast(fp32), ALU.subtract)
                nc.vector.tensor_tensor(out_lo[:, l, :], out_scaled[:, l, :], out_hi[:, l, :].bitcast(fp32), ALU.subtract)
                nc.vector.tensor_tensor(gate_lo[:, l, 0:e], gate_raw[:, l, 0:e], gate_hi[:, l, 0:e].bitcast(fp32),
                                        ALU.subtract).then_inc(s_conv_w, 1)

            def out_bias_ready(l):
                dve.wait_ge(s_outb, LAYERS)
                nc.vector.tensor_tensor(out_bias[:, l:l + 1], DOWN[0:D, l:l + 1], column(l, OUT_B, D),
                                        ALU.add).then_inc(s_outb_ready, 1)

            def make_moments(n, src):
                for t in range(TILES):
                    last = nc.vector.bn_stats(stats[n][:, t, :], src[:, t, :])
                link(last)
                for t in range(TILES):
                    last = nc.vector.bn_aggr(moments[n][:, t, :], stats[n][:, t, :])
                last.then_inc(s_stats[n], 1)

            def make_parts(n, count, src):
                dve.wait_ge(s_rstd[n], count)
                dve.wait_ge(s_stats[n], count)
                if count > 1:
                    dve.wait_ge(s_turn[n], count - 1)
                for t in range(TILES):
                    last = nc.vector.tensor_scalar(norm[n][:, t, :], src[:, t, :], moments[n][:, t, 0:1],
                                                   rstd[n][:, t:t + 1], ALU.subtract, ALU.mult)
                link(last)
                link(nc.vector.tensor_copy(parts[n][:, :, 0, :].bitcast(fp32r), norm[n][:, :, :]))
                nc.vector.tensor_tensor(parts[n][:, :, 1, :], norm[n][:, :, :], parts[n][:, :, 0, :],
                                        ALU.subtract).then_inc(s_parts[n], 1)

            def group_rows(u):
                return rows[:, u % GROUPS, :, :, :].rearrange("p i f d -> p (i f) d")

            def conv(u, k):
                l = layer(u)
                if k == 0:
                    if u < GROUPS:
                        dve.wait_ge(s_x[u], 16 * HALF)
                    else:
                        dve.wait_ge(s_exit, u - GROUPS + 1)
                    make_moments("c", group_rows(u))
                elif k == 1:
                    make_parts("c", 2 * u + 1, group_rows(u))
                elif k == 4:
                    dve.wait_ge(s_sig, u + 1)
                    dve.wait_ge(s_proj, 3 * u + 2)
                    link(nc.vector.scalar_tensor_tensor(silu_i[:, :], M0[:, :], column(l, I_B),
                                                        sig_i[:, :], ALU.add, ALU.mult))
                    if u == 0:
                        dve.wait_ge(s_pads, 1)
                    else:
                        dve.wait_ge(s_add_h, u)
                    nc.vector.scalar_tensor_tensor(by_image(body(add_w)), by_image(body(lam_w)), 1.0,
                                                   square(silu_i[:, :]), ALU.subtract, ALU.mult).then_inc(s_add_w, 1)
                elif k == 5:
                    dve.wait_ge(s_add_w, u + 1)
                    if u:
                        dve.wait_ge(s_sum_w, u)
                    nc.vector.tensor_tensor_scan(fwd_w[:, 0:SCAN - 1], lam_w[:, 0:SCAN - 1], add_w[:, 0:SCAN - 1],
                                                 0.0, ALU.mult, ALU.add)
                    nc.vector.tensor_tensor_scan(rev_w[:, SCAN - 1:0:-1], lam_w[:, SCAN - 1:0:-1],
                                                 add_w[:, SCAN - 1:0:-1], 0.0, ALU.mult, ALU.add).then_inc(s_scan_w, 1)
                elif k == 6:
                    dve.wait_ge(s_add_h, u + 1)
                    nc.vector.tensor_tensor_scan(fwd_h[:, 0:SCAN - 1], lam_h[:, 0:SCAN - 1], add_h[:, 0:SCAN - 1],
                                                 0.0, ALU.mult, ALU.add)
                    nc.vector.tensor_tensor_scan(rev_h[:, SCAN - 1:0:-1], lam_h[:, SCAN - 1:0:-1],
                                                 add_h[:, SCAN - 1:0:-1], 0.0, ALU.mult, ALU.add).then_inc(s_scan_h, 1)
                elif k == 7:
                    dve.wait_ge(s_scan_h, u + 1)
                    link(nc.vector.tensor_tensor(square(sum_h[:, :]), turned(body(fwd_h)), turned(body(rev_h)), ALU.add))
                    dve.wait_ge(s_sum_w, u + 1)
                    link(nc.vector.tensor_tensor(sum_h[:, :], sum_h[:, :], sum_w[:, :], ALU.add))
                    dve.wait_ge(s_tanh_o, u + 1)
                    if u:
                        dve.wait_ge(s_gturn, u)
                    nc.vector.scalar_tensor_tensor(gated[:, :], tanh_o[:, :], 1.0, sum_h[:, :],
                                                   ALU.add, ALU.mult).then_inc(s_gated, 1)
                elif k == 8:
                    dve.wait_ge(s_gturn, u + 1)
                    nc.vector.tensor_reduce(
                        heads[:, :, :].rearrange("p t (h e) -> p (t h) e", e=2),
                        M0[:, :].rearrange("p (t h d e) -> p (t h) e d", t=TILES, d=2, e=2),
                        mybir.AxisListType.X, ALU.add).then_inc(s_heads, 1)
                    dve.wait_ge(s_heads, u + 1)
                    make_moments("c", heads)
                elif k == 9:
                    make_parts("c", 2 * u + 2, heads)
                elif k == 12:
                    dve.wait_ge(s_yturn, u + 1)
                    r = group_rows(u)
                    nc.vector.tensor_tensor(r, r, M1[:, 0:TILES * D].rearrange("p (t d) -> p t d", t=TILES),
                                            ALU.add).then_inc(s_conv, 1)

            def entry(u, k):
                l = layer(u)
                e = EXPERTS[l]
                if k == 0:
                    dve.wait_ge(s_conv, u + 1)
                    make_moments("e", group_rows(u))
                elif k == 1:
                    make_parts("e", u + 1, group_rows(u))
                elif k == 4:
                    dve.wait_ge(s_lgturn, u + 1)
                    if u == 0:
                        dve.wait_ge(s_const, 2)
                        nc.vector.tensor_copy(iota[:, :], iota_i[:, :])
                    link(nc.vector.tensor_copy(logits[:, :, 0:e], M2[:, 0:TILES * e].rearrange("p (t e) -> p t e", t=TILES)))
                    for t in range(TILES):
                        last = nc.vector.max(best[:, t, :], logits[:, t, 0:e])
                    link(last)
                    nc.vector.tensor_tensor(margin[:, :], best[:, :, 0], best[:, :, 1], ALU.subtract).then_inc(s_margin, 1)
                    for t in range(TILES):
                        last = nc.vector.max_index(best_at[:, t, :], best[:, t, :], logits[:, t, 0:e])
                    link(last)
                    link(nc.vector.tensor_copy(best_atf[:, :, :], best_at[:, :, 0:2]))
                    for k2 in range(2):
                        last = nc.vector.tensor_tensor(
                            pick[:, k2, :, 0:e], iota[:, 0:e].unsqueeze(1).broadcast_to([P, TILES, e]),
                            best_atf[:, :, k2:k2 + 1].broadcast_to([P, TILES, e]), ALU.is_equal)
                    last.then_inc(s_lgread, 1)
                elif k == 6:
                    dve.wait_ge(s_tm, u + 1)
                    nc.vector.tensor_scalar(shares[:, :, 0], tanh_m[:, :], 0.5, 0.5, ALU.mult, ALU.add)
                    link(nc.vector.tensor_scalar(shares[:, :, 1], tanh_m[:, :], -0.5, 0.5, ALU.mult, ALU.add))
                    dve.wait_ge(s_lgread, u + 1)
                    for k2 in range(2):
                        last = nc.vector.tensor_tensor(pick[:, k2, :, 0:e], pick[:, k2, :, 0:e],
                                                       shares[:, :, k2:k2 + 1].broadcast_to([P, TILES, e]), ALU.mult)
                    link(last)
                    if u:
                        dve.wait_ge(s_gateturn, u)
                    nc.vector.tensor_tensor(gates[:, :, 0:e], pick[:, 0, :, 0:e], pick[:, 1, :, 0:e],
                                            ALU.add).then_inc(s_gates, 1)

            def leave(u, k):
                if k == 1:
                    dve.wait_ge(s_xturn, u + 1)
                    dve.wait_ge(s_conv, u + 1)
                    r = group_rows(u)
                    m = tiles(M2[:, :])
                    link(nc.vector.tensor_tensor(r, r, m[:, :, 0:D], ALU.add))
                    nc.vector.tensor_tensor(r, r, m[:, :, D:P], ALU.add).then_inc(s_exit, 1)

            def step(u, i):
                if layer(u):
                    return
                n = steps_before(u) + i
                dve.wait_ge(s_silu_h, n + 1)
                dve.wait_ge(s_upb, n + 1)
                if n >= 4:
                    dve.wait_ge(s_dn, (n - 4) // 2 + 1)
                nc.vector.tensor_tensor(hidden[:, n % 4, 0, :], silu_h[:, n % 2, :], UP[:, 2 * (n % 2) + 1, :],
                                        ALU.mult).then_inc(s_hid0, 1)

            def weigh_pair(u, i):
                q = pairs_before(u) + i
                dve.wait_ge(s_dn, q + 1)
                g = gates_b[:, u % 2, i, :]
                if i == 0:
                    dve.wait_ge(s_gback[u % 2], 32 * (u // 2 + 1))
                    if u >= 2:
                        dve.wait_ge(s_xturn, u - 1)
                    dst = total[:, u % 2, :]
                else:
                    dst = weighted[:, q % 2, :]
                    if i > 2:
                        dve.wait_ge(s_sum, adds_before(u) + i - 2)
                    elif u:
                        dve.wait_ge(s_sum, adds_before(u))
                if layer(u) == 0:
                    nc.vector.tensor_tensor(dst, DOWN[:, :], g, ALU.mult).then_inc(s_pm, 1)
                else:
                    nc.vector.scalar_tensor_tensor(dst, DOWN[:, :], columns[:, 16 + i:17 + i], g,
                                                   ALU.add, ALU.mult).then_inc(s_pm, 1)

            def stages(slot):
                for part, u, k in slot:
                    if part == "C":
                        conv(u, k)
                    elif part == "E":
                        entry(u, k)
                    else:
                        leave(u, k)

            dve.wait_ge(s_vturn, 1)
            nc.vector.tensor_copy(columns[:, :], DOWN[:, 0:20 + 7 * LAYERS]).then_inc(s_columns, 1)
            dve.wait_ge(s_columns, 1)
            conv_weights(0)
            for j, slot in enumerate(before):
                if j == 5:
                    conv_weights(1)
                    for l in range(LAYERS):
                        out_bias_ready(l)
                stages(slot)
            for u in range(UNITS):
                for i, slot in each_slot(u):
                    step(u, i)
                    if i % 2 == 0:
                        if i >= 4:
                            weigh_pair(u, i // 2 - 2)
                        elif u:
                            weigh_pair(u - 1, PAIRS[layer(u - 1)] + i // 2 - 2)
                    stages(slot)
            for i in (-2, -1):
                weigh_pair(UNITS - 1, PAIRS[1] + i)
            leave(UNITS - 1, 1)

        @block.tensor
        def _(pe):
            def product(dst, hi, lo, z):
                nc.tensor.matmul(dst, hi, z, start=True, stop=False)
                return nc.tensor.matmul(dst, lo, z, start=False, stop=True)

            def turn(dst, src, k=P):
                return nc.tensor.transpose(dst, src, ident[0:k, 0:k])

            def small_products():
                pe.wait_ge(s_columns, 1)
                for l in range(LAYERS):
                    pe.wait_ge(s_small[l], 16 * 6)
                    nc.tensor.matmul(DOWN[0:D, l:l + 1], out_raw[0:D, l, :], column(l, BETA, D),
                                     start=True, stop=True).then_inc(s_outb, 1)

            def turn_parts(n, count, dst):
                pe.wait_ge(s_parts[n], count)
                for t in range(TILES):
                    last = turn(dst[:, t * P:(t + 1) * P], parts[n][:, t, :, :].rearrange("p k d -> p (k d)"))
                last.then_inc(s_turn[n], 1)

            def wait_m2(part, u):
                if m2_before[part, u]:
                    was, v = m2_before[part, u]
                    pe.wait_ge(s_gatec if was == "E" else s_exit, v + 1)

            def conv(u, k):
                l = layer(u)
                if k == 2:
                    if u:
                        pe.wait_ge(s_yc, u)
                    turn_parts("c", 2 * u + 1, M0)
                elif k == 3:
                    pe.wait_ge(s_z["c"], 2 * u + 1)
                    if u:
                        pe.wait_ge(s_conv, u)
                    if u in (0, GROUPS):
                        pe.wait_ge(s_conv_w, l + 1)
                    for dst, which in ((M1, FORGET), (M0, INPUT)):
                        product(dst[:, :], in_hi[:, l, which, :], in_lo[:, l, which, :], conv_z[:, :]).then_inc(s_proj, 1)
                elif k == 4:
                    pe.wait_ge(s_tanh_f, u + 1)
                    product(M1[:, :], in_hi[:, l, OUTPUT, :], in_lo[:, l, OUTPUT, :], conv_z[:, :]).then_inc(s_proj, 1)
                elif k == 8:
                    pe.wait_ge(s_gated, u + 1)
                    pe.wait_ge(s_add_w, u + 1)
                    for t in range(TILES):
                        last = turn(M0[:, t * P:(t + 1) * P], gated[:, t * P:(t + 1) * P])
                    last.then_inc(s_gturn, 1)
                elif k == 10:
                    pe.wait_ge(s_tanh_o, u + 1)
                    turn_parts("c", 2 * u + 2, M1)
                elif k == 11:
                    pe.wait_ge(s_z["c"], 2 * u + 2)
                    pe.wait_ge(s_heads, u + 1)
                    product(M0[0:D, :], out_hi[:, l, :], out_lo[:, l, :], conv_z[:, :]).then_inc(s_y, 1)
                elif k == 12:
                    pe.wait_ge(s_yc, u + 1)
                    for t in range(TILES):
                        last = turn(M1[:, t * D:(t + 1) * D], conv_y[:, t * P:(t + 1) * P], D)
                    last.then_inc(s_yturn, 1)

            def entry(u, k):
                l = layer(u)
                e = EXPERTS[l]
                if k == 2:
                    wait_m2("E", u)
                    turn_parts("e", u + 1, M2)
                elif k == 3:
                    pe.wait_ge(s_z["e"], u + 1)
                    product(M2[0:e, :], gate_hi[:, l, 0:e], gate_lo[:, l, 0:e], tok_z[:, u % 2, :]).then_inc(s_lg, 1)
                elif k == 4:
                    pe.wait_ge(s_lgc, u + 1)
                    for t in range(TILES):
                        last = turn(M2[:, t * e:(t + 1) * e], logits_t[0:e, t * P:(t + 1) * P], e)
                    last.then_inc(s_lgturn, 1)
                elif k == 7:
                    pe.wait_ge(s_gates, u + 1)
                    for t in range(TILES):
                        last = turn(M2[0:e, t * P:(t + 1) * P], gates[:, t, 0:e])
                    last.then_inc(s_gateturn, 1)

            def leave(u, k):
                if k == 0:
                    pe.wait_ge(s_sum, adds_before(u + 1))
                    wait_m2("X", u)
                    for t in range(TILES):
                        last = turn(M2[:, t * P:(t + 1) * P], total[:, u % 2, t * P:(t + 1) * P])
                    last.then_inc(s_xturn, 1)

            def up(u, i):
                n = steps_before(u) + i
                a = 2 * (n % 2)
                if i == 0:
                    pe.wait_ge(s_z["e"], u + 1)
                if n >= 2:
                    wait_hidden(pe, n - 2)
                if i % 2 == 0 and u in (0, GROUPS):
                    pe.wait_ge(s_split, 8 * layer(u) + i // 2 + 1)
                hi, lo = (up_hi1, up_lo1) if layer(u) else (up_hi0, up_lo0)
                z = tok_z[:, u % 2, :]
                product(UP[:, a, :], hi[:, i, 0, :], lo[:, i, 0, :], z).then_inc(s_upa, 1)
                product(UP[:, a + 1, :], hi[:, i, 1, :], lo[:, i, 1, :], z).then_inc(s_upb, 1)

            def down(u, i):
                q = pairs_before(u) + i
                wait_hidden(pe, 2 * q + 1)
                if q:
                    pe.wait_ge(s_pm, q)
                else:
                    pe.wait_ge(s_outb_ready, 2)
                if i == 0 and u in (0, GROUPS):
                    pe.wait_ge(s_down[layer(u)], 16)
                chunks = 1 + layer(u)
                for j in range(chunks):
                    for k in range(2):
                        w = down1[:, 2 * i + k, j, :] if layer(u) else down0[:, 2 * i + k, :]
                        last = nc.tensor.matmul(DOWN[k * D:(k + 1) * D, :], w, hidden[:, (2 * q + k) % 4, j, :],
                                                start=(j == 0), stop=(j == chunks - 1))
                last.then_inc(s_dn, 1)

            def stages(slot):
                for part, u, k in slot:
                    if part == "C":
                        conv(u, k)
                    elif part == "E":
                        entry(u, k)
                    else:
                        leave(u, k)

            pe.wait_ge(s_const, 1)
            pe.wait_ge(s_vectors, 16 * (2 + 10 * LAYERS))
            turn(DOWN[:, 0:20 + 7 * LAYERS], vectors[:, :], 20 + 7 * LAYERS).then_inc(s_vturn, 1)
            for j, slot in enumerate(before):
                if j == 5:
                    small_products()
                stages(slot)
            for u in range(UNITS):
                for i, slot in each_slot(u):
                    up(u, i)
                    if i % 2:
                        if i >= LAG:
                            down(u, (i - LAG) // 2)
                        elif u:
                            down(u - 1, PAIRS[layer(u - 1)] - 1)
                    stages(slot)
            down(UNITS - 1, PAIRS[1] - 1)
            leave(UNITS - 1, 0)


_INS = ['x', 'L0_conv_in_w', 'L0_conv_in_b', 'L0_conv_out_w', 'L0_conv_out_b', 'L0_conv_gamma', 'L0_conv_beta',
        'L0_ffn_gate_w', 'L0_ffn_gate_b', 'L0_ffn_w1', 'L0_ffn_w2', 'L0_ffn_w3',
        'L1_conv_in_w', 'L1_conv_in_b', 'L1_conv_out_w', 'L1_conv_out_b', 'L1_conv_gamma', 'L1_conv_beta',
        'L1_ffn_Wg', 'L1_ffn_bg', 'L1_ffn_W1', 'L1_ffn_b1', 'L1_ffn_W2', 'L1_ffn_b2']


def kernel(**inputs):
    import numpy as _np
    import concourse.bacc as _bacc
    from concourse import mybir as _mybir
    from concourse.bass_utils import run_bass_kernel_spmd as _run

    nc = _bacc.Bacc("TRN2", target_bir_lowering=False, num_devices=1)
    arrays, args = {}, []
    for name in _INS:
        a = _np.ascontiguousarray(inputs[name])
        arrays[f"in_{name}_dram"] = a
        args.append(nc.dram_tensor(f"in_{name}_dram", a.shape, _mybir.dt.from_np(a.dtype), kind="ExternalInput").ap())
    args.append(nc.dram_tensor("out_dram", (H, W, B, D), _mybir.dt.float32, kind="ExternalOutput").ap())
    metaformer(nc, *args)
    r = _run(nc, [arrays], core_ids=[0])
    return r.results[0]["out_dram"]
```

```python
import concourse.bass as bass
from concourse import mybir
from contextlib import ExitStack

H, W, B, D = 16, 16, 8, 64
P = 128
GB = 2
GROUPS = B // GB
LAYERS = 2
UNITS = LAYERS * GROUPS
TOK = GB * H * W
HALF = H * W // P
TILES = GB * HALF
SEQ = 16
NSEQ = TOK // SEQ
PAD = SEQ + 1
SCAN = NSEQ * PAD + 1
EXPERTS = (16, 8)
STEPS = EXPERTS
PAIRS = tuple(e // 2 for e in EXPERTS)
HID = 128
EPS_C = 1e-6
EPS_T = 1e-5
SCALE = -8.0
LAG = 3


def layer(u):
    return u // GROUPS


def steps_before(u):
    return sum(STEPS[layer(v)] for v in range(u))


def pairs_before(u):
    return steps_before(u) // 2


def adds_before(u):
    return pairs_before(u) - u


UP_CHUNKS = ((0, 0, 4), (0, 4, 16), (1, 0, 8))

SLOTS = 16
A_STAGES, B_STAGES, E_STAGES, X_STAGES = 12, 9, 11, 2
A_PERIOD = 8
BEFORE = A_STAGES + B_STAGES + 5
X_FROM = 8


def chunk(pair):
    l, e = pair // PAIRS[0], 2 * (pair % PAIRS[0])
    return next(c for c, (layer_, first, end) in enumerate(UP_CHUNKS) if layer_ == l and first <= e < end)


def schedule():
    slots = [(-1, j) for j in range(BEFORE)] + [(u, j) for u in range(UNITS) for j in range(SLOTS)]
    plan, me_before, me_last = {}, {}, None
    a = [0] * UNITS
    b, e, x = list(a), list(a), list(a)

    def first(done, stages):
        return next((v for v in range(UNITS) if done[v] < stages), UNITS)

    for u, j in slots:
        here = []
        a_was, b_was, e_was, x_was = list(a), list(b), list(e), list(x)
        for v in range(UNITS):
            if a[v] == A_STAGES or (v and not a[v] and a_was[v - 1] < A_PERIOD):
                continue
            if v >= GROUPS and x_was[v - GROUPS] < X_STAGES:
                continue
            here.append(("A", v, a[v]))
            a[v] += 1
        v = first(b, B_STAGES)
        if v < UNITS and a_was[v] == A_STAGES:
            here.append(("B", v, b[v]))
            b[v] += 1
        v, w = first(e, E_STAGES), first(x, X_STAGES)
        x_open = w == u - 1 and j >= X_FROM
        e_open = v < UNITS and v <= u + 1 and b_was[v] == B_STAGES
        if x[w] if w < UNITS else 0:
            x_goes = True
        else:
            x_goes = x_open and not (e_open and e[v])
        if x_goes:
            if not x[w]:
                me_before["X", w], me_last = me_last, ("X", w)
            here.append(("X", w, x[w]))
            x[w] += 1
        elif e_open:
            for _ in range(E_STAGES - e[v] if j == SLOTS - 1 and v == u + 1 else 1):
                if not e[v]:
                    me_before["E", v], me_last = me_last, ("E", v)
                here.append(("E", v, e[v]))
                e[v] += 1
        if (u, j) == (-1, BEFORE - 1):
            while e[0] < E_STAGES:
                if not e[0]:
                    me_before["E", 0], me_last = me_last, ("E", 0)
                here.append(("E", 0, e[0]))
                e[0] += 1
        plan[u, j] = here
        if j == SLOTS - 1 and u + 1 < UNITS and u >= 0:
            assert e[u + 1] == E_STAGES, (u, e)
    me_before["X", UNITS - 1] = me_last
    assert first(a, A_STAGES) == first(b, B_STAGES) == first(e, E_STAGES) == UNITS and first(x, X_STAGES) == UNITS - 1
    return ([plan[-1, j] for j in range(BEFORE)], [[plan[u, j] for j in range(SLOTS)] for u in range(UNITS)],
            me_before)


def metaformer(nc, x, L0_conv_in_w, L0_conv_in_b, L0_conv_out_w, L0_conv_out_b, L0_conv_gamma, L0_conv_beta,
               L0_ffn_gate_w, L0_ffn_gate_b, L0_ffn_w1, L0_ffn_w2, L0_ffn_w3,
               L1_conv_in_w, L1_conv_in_b, L1_conv_out_w, L1_conv_out_b, L1_conv_gamma, L1_conv_beta,
               L1_ffn_Wg, L1_ffn_bg, L1_ffn_W1, L1_ffn_b1, L1_ffn_W2, L1_ffn_b2, out):
    fp32, fp32r = mybir.dt.float32, mybir.dt.float32r
    i32, u32 = mybir.dt.int32, mybir.dt.uint32
    ALU = mybir.AluOpType
    ACT = mybir.ActivationFunctionType

    conv_in_w, conv_in_b = (L0_conv_in_w, L1_conv_in_w), (L0_conv_in_b, L1_conv_in_b)
    conv_out_w, conv_out_b = (L0_conv_out_w, L1_conv_out_w), (L0_conv_out_b, L1_conv_out_b)
    gamma, beta = (L0_conv_gamma, L1_conv_gamma), (L0_conv_beta, L1_conv_beta)
    gate_w, gate_b = (L0_ffn_gate_w, L1_ffn_Wg), (L0_ffn_gate_b, L1_ffn_bg)
    x_rows = x.rearrange("h w (g i) d -> (h w) g i d", g=GROUPS)
    out_rows = out.rearrange("h w (g i) d -> (h w) g i d", g=GROUPS)

    before, beside, me_before = schedule()

    ctx = ExitStack()
    with ctx:
        def sb(name, shape, dt=fp32):
            return ctx.enter_context(nc.sbuf_tensor(name, shape, dt))

        def sem(name):
            return ctx.enter_context(nc.semaphore(name))

        ident = sb("ident", [P, P])
        iota_i = sb("iota_i", [P, 16], i32)
        iota = sb("iota", [P, 16])
        minus_half = sb("minus_half", [P, TILES])
        rows = sb("rows", [P, GROUPS, GB, HALF, D])
        in_raw = sb("in_raw", [P, LAYERS, 3 * D])
        in_wide = sb("in_wide", [P, 3, P])
        in_hi = sb("in_hi", [P, LAYERS, 3, P], fp32r)
        in_lo = sb("in_lo", [P, LAYERS, 3, P], fp32r)
        out_raw = sb("out_raw", [P, LAYERS, D])
        out_scaled = sb("out_scaled", [P, LAYERS, D])
        out_hi = sb("out_hi", [P, LAYERS, D], fp32r)
        out_lo = sb("out_lo", [P, LAYERS, D], fp32r)
        gate_raw = sb("gate_raw", [P, LAYERS, 16])
        gate_hi = sb("gate_hi", [P, LAYERS, 16], fp32r)
        gate_lo = sb("gate_lo", [P, LAYERS, 16], fp32r)
        vectors = sb("vectors", [LAYERS, 6 * D + 16])
        wide = sb("wide", [LAYERS, 7, P])
        columns = sb("columns", [P, 7, LAYERS])
        half_bias = sb("half_bias", [P, 3, LAYERS])
        expert_rows = sb("expert_rows", [20, P])
        expert_bias = sb("expert_bias", [P, 20])
        out_bias = sb("out_bias", [D, LAYERS])
        up_raw = sb("up_raw", [P, 16, 2, HID])
        up_hi0 = sb("up_hi0", [P, 16, 2, HID], fp32r)
        up_lo0 = sb("up_lo0", [P, 16, 2, HID], fp32r)
        up_hi1 = sb("up_hi1", [P, 8, 2, HID], fp32r)
        up_lo1 = sb("up_lo1", [P, 8, 2, HID], fp32r)
        down0 = sb("down0", [P, 16, D])
        down1 = sb("down1", [P, 8, 2, D])
        stats = {n: sb(f"stats_{n}", [P, TILES, 6]) for n in "abe"}
        moments = {n: sb(f"moments_{n}", [P, TILES, 2]) for n in "abe"}
        spread = {n: sb(f"spread_{n}", [P, TILES]) for n in "abe"}
        rstd = {n: sb(f"rstd_{n}", [P, TILES]) for n in "abe"}
        shift = {n: sb(f"shift_{n}", [P, TILES]) for n in "abe"}
        norm = {n: sb(f"norm_{n}", [P, TILES, D]) for n in "abe"}
        parts = {n: sb(f"parts_{n}", [P, TILES, 2, D]) for n in "abe"}
        conv_z = sb("conv_z", [P, TOK], fp32r)
        tanh_f = sb("tanh_f", [P, TOK])
        tanh_i = sb("tanh_i", [P, TOK])
        tanh_o = sb("tanh_o", [P, TOK])
        value_i = sb("value_i", [P, TOK])
        lam_w = sb("lam_w", [P, SCAN])
        lam_h = sb("lam_h", [P, SCAN])
        add_w = sb("add_w", [P, SCAN])
        add_h = sb("add_h", [P, SCAN])
        fwd_w, rev_w, fwd_h, rev_h = (sb(n, [P, SCAN]) for n in ("fwd_w", "rev_w", "fwd_h", "rev_h"))
        gated = sb("gated", [P, TOK])
        heads = sb("heads", [P, TILES, D])
        heads_z = sb("heads_z", [P, TOK], fp32r)
        conv_y = sb("conv_y", [D, TOK])
        tok_z = sb("tok_z", [P, 2, TOK], fp32r)
        logits_t = sb("logits_t", [16, TOK])
        logits = sb("logits", [P, TILES, 16])
        best = sb("best", [P, TILES, 8])
        best_at = sb("best_at", [P, TILES, 8], u32)
        best_atf = sb("best_atf", [P, TILES, 2])
        margin = sb("margin", [P, TILES])
        tanh_m = sb("tanh_m", [P, TILES])
        shares = sb("shares", [P, TILES, 2])
        pick = sb("pick", [P, 2, TILES, 16])
        gates = sb("gates", [P, TILES, 16])
        gates_t = sb("gates_t", [16, TOK])
        gates_b = sb("gates_b", [P, 2, 8, TOK])
        silu_h = sb("silu_h", [P, 2, TOK])
        hidden = sb("hidden", [P, 4, 2, TOK])
        weighted = sb("weighted", [P, 2, TOK])
        total = sb("total", [P, 2, TOK])

        gates_dram = nc.dram_tensor("gates_dram", (UNITS, 16, TOK), fp32, kind="Internal").ap()

        UP = ctx.enter_context(nc.psum_tensor("UP", [P, 4, TOK], fp32))
        DOWN = ctx.enter_context(nc.psum_tensor("DOWN", [P, TOK], fp32))
        MA, MB, ME = (ctx.enter_context(nc.psum_tensor(n, [P, TOK], fp32)) for n in ("MA", "MB", "ME"))

        F_B, O_B, I_B, GAMMA, BETA, OUT_B, GATE_B = range(7)

        def column(l, which, n=P):
            return columns[0:n, which, l:l + 1]

        FORGET, INPUT, OUTPUT = range(3)

        def tiles(t):
            return t.rearrange("p (t n) -> p t n", t=TILES)

        def body(t):
            return t[:, 0:NSEQ * PAD].rearrange("p (s n) -> p s n", n=PAD)[:, :, 1:PAD]

        def by_image(ap):
            return ap.rearrange("p (i s) n -> p i s n", i=GB)

        def turned(ap):
            return ap.rearrange("p (i s) n -> p i n s", i=GB)

        def square(t):
            return t.rearrange("p (i s n) -> p i s n", i=GB, s=H)

        s_x = [sem("rows_loaded_first"), sem("rows_loaded_others")]
        s_small = [sem(f"conv_weights_loaded{l}") for l in range(LAYERS)]
        s_up = [sem(f"up_loaded{c}") for c in range(len(UP_CHUNKS))]
        s_down = [sem(f"down_loaded{l}") for l in range(LAYERS)]
        s_vectors = sem("vectors_loaded")
        s_expert_rows = sem("expert_rows_loaded")
        s_zeroed = sem("vector_rows_zeroed")
        s_const = sem("constants_ready")
        s_pads = sem("pads_zeroed")
        s_wide = sem("vectors_widened")
        s_outb = sem("out_bias_products_and_expert_turn")
        s_expert_bias = sem("expert_bias_ready")
        s_outb_ready = sem("out_bias_ready")
        s_conv_w = sem("conv_weights_split")
        s_hi = sem("up_high_parts")
        s_split = sem("up_pairs_split")
        s_vturn = sem("vectors_turned")
        s_columns = sem("columns_ready")
        s_dve = sem("vector_chain")
        s_pool = sem("pool_chain")
        s_stats = {n: sem(f"moments_ready_{n}") for n in "abe"}
        s_rstd = {n: sem(f"rstd_ready_{n}") for n in "abe"}
        s_norm = {n: sem(f"normalised_{n}") for n in "abe"}
        s_parts = {n: sem(f"norm_parts_ready_{n}") for n in "abe"}
        s_turn = {n: sem(f"norm_turned_{n}") for n in "abe"}
        s_z = {n: sem(f"norm_columns_ready_{n}") for n in "abe"}
        s_proj = sem("projections_done")
        s_tanh_f = sem("tanh_f_ready")
        s_value = sem("value_i_ready")
        s_tanh_o = sem("tanh_o_ready")
        s_lam = sem("lambdas_ready")
        s_add_w = sem("row_inputs_ready")
        s_add_h = sem("column_inputs_ready")
        s_scan_w = sem("row_scans_done")
        s_scan_h = sem("column_scans_done")
        s_sum_w = sem("row_scans_summed")
        s_sum_h = sem("column_scans_summed")
        s_gated = sem("gated_ready")
        s_gturn = sem("gated_turned")
        s_heads = sem("heads_ready")
        s_y = sem("conv_output_product")
        s_yc = sem("conv_output_copied")
        s_yturn = sem("conv_output_turned")
        s_conv = sem("conv_residual_done")
        s_lg = sem("logits_product")
        s_lgc = sem("logits_copied")
        s_lgturn = sem("logits_turned")
        s_margin = sem("margin_ready")
        s_lgread = sem("logits_read")
        s_tm = sem("margin_tanh")
        s_gates = sem("gates_ready")
        s_gateturn = sem("gates_turned")
        s_gatec = sem("gates_copied")
        s_gsent = [sem(f"gates_sent{k}") for k in range(2)]
        s_gback = [sem(f"gates_broadcast{k}") for k in range(2)]
        s_upa = sem("up_first_bank")
        s_upb = sem("up_second_bank")
        s_silu_h = sem("silu_ready")
        s_hid0 = sem("hidden_ready0")
        s_hid1 = sem("hidden_ready1")
        s_dn = sem("pair_down_done")
        s_pm = sem("pair_weighted")
        s_sum = sem("pair_added")
        s_xturn = sem("total_turned")
        s_exit = sem("exit_residual_done")
        s_out = sem("rows_stored")

        N0 = steps_before(GROUPS)

        def wait_hidden(eng, n):
            if n < N0:
                eng.wait_ge(s_hid0, n + 1)
            else:
                eng.wait_ge(s_hid1, n + 1 - N0)

        def each_slot(u):
            per = SLOTS // STEPS[layer(u)]
            for i in range(STEPS[layer(u)]):
                yield i, [s for j in range(per) for s in beside[u][per * i + j]]

        def group_rows(u):
            return rows[:, u % GROUPS, :, :, :].rearrange("p i f d -> p (i f) d")

        def wait_up(eng, pair):
            eng.wait_ge(s_up[chunk(pair)], 64 if pair < PAIRS[0] else 32)

        block = ctx.enter_context(nc.Block())

        @block.sync
        def _(sp):
            def load_rows(first, end, s):
                for half in range(HALF):
                    sp.dma_start(rows[:, first:end, :, half, :],
                                 x_rows[half * P:(half + 1) * P, first:end, :, :]).then_inc(s, 16)

            def load_up(c):
                l, first, end = UP_CHUNKS[c]
                e = slice(first, end)
                for k in range(2):
                    part = slice(k * D, (k + 1) * D)
                    if l == 0:
                        for n, w in enumerate((L0_ffn_w1, L0_ffn_w2)):
                            sp.dma_start(up_raw[part, e, n, :], w[e, :, :].rearrange("e d h -> d e h")).then_inc(s_up[c], 16)
                    else:
                        sp.dma_start(up_raw[part, e, :, :],
                                     L1_ffn_W1[e, :, :].rearrange("e d (j h) -> d e j h", j=2)).then_inc(s_up[c], 16)

            load_rows(0, 1, s_x[0])
            load_up(0)
            load_rows(1, GROUPS, s_x[1])
            load_up(1)
            sp.dma_start(down0[:, :, :], L0_ffn_w3.rearrange("e h o -> h e o")).then_inc(s_down[0], 16)
            sp.dma_start(down1[:, :, :, :], L1_ffn_W2.rearrange("e (j h) o -> h e j o", j=2)).then_inc(s_down[1], 16)
            sp.dma_start(expert_rows[0:16, :], L1_ffn_b1.rearrange("e (j h) -> (e j) h", j=2)).then_inc(s_expert_rows, 16)
            sp.dma_start(expert_rows[16:20, :], L1_ffn_b2.rearrange("(q k) o -> q (k o)", k=2)).then_inc(s_expert_rows, 16)

            def load_up1():
                sp.wait_ge(s_split, PAIRS[0])
                load_up(2)

            def broadcast_gates(u):
                sp.wait_ge(s_gatec, u + 1)
                e = EXPERTS[layer(u)]
                sp.dma_start(gates_dram[u, 0:e, :], gates_t[0:e, :]).then_inc(s_gsent[u % 2], 16)
                sp.wait_ge(s_gsent[u % 2], 16 * (u // 2 + 1))
                if u >= 2:
                    sp.wait_ge(s_pm, pairs_before(u - 1))
                by_pair = gates_dram[u, 0:e, :].rearrange("(q k) n -> k q n", k=2)
                for k in range(2):
                    sp.dma_start(gates_b[k * D:(k + 1) * D, u % 2, 0:e // 2, :],
                                 by_pair[k:k + 1, :, :].broadcast_to([D, e // 2, TOK])).then_inc(s_gback[u % 2], 16)

            def store_rows(u):
                g = u % GROUPS
                sp.wait_ge(s_exit, u + 1)
                for half in range(HALF):
                    sp.dma_start(out_rows[half * P:(half + 1) * P, g, :, :], rows[:, g, :, half, :]).then_inc(s_out, 16)

            for u in range(UNITS):
                broadcast_gates(u)
                if u == 0:
                    load_up1()
                if u >= GROUPS + 2:
                    store_rows(u - 2)
            for u in (UNITS - 2, UNITS - 1):
                store_rows(u)
            sp.wait_ge(s_out, 16 * HALF * GROUPS)

        @block.gpsimd
        def _(pool):
            chain = [0]

            def link(ins):
                chain[0] += 1
                ins.then_inc(s_pool, 1)
                pool.wait_ge(s_pool, chain[0])

            nc.gpsimd.memset(vectors[:, :], 0.0).then_inc(s_zeroed, 1)
            link(nc.gpsimd.memset(ident[:, :], 0.0))
            nc.gpsimd.affine_select(out=ident[:, :], in_=ident[:, :], compare_op=ALU.not_equal, fill=1.0, base=0,
                                    pattern=[[-1, P]], channel_multiplier=1).then_inc(s_const, 1)
            nc.gpsimd.iota(iota_i[:, :], [[1, 16]], base=0, channel_multiplier=0).then_inc(s_const, 1)
            link(nc.gpsimd.memset(minus_half[:, :], -0.5))
            nc.gpsimd.memset(wide[:, GATE_B, :], 0.0).then_inc(s_zeroed, 1)
            for t in (lam_w, lam_h, add_w, add_h):
                last = nc.gpsimd.memset(t[:, 0:SCAN:PAD], 0.0)
            last.then_inc(s_pads, 1)

            def make_rstd(n, u, eps):
                pool.wait_ge(s_stats[n], u + 1)
                if u:
                    pool.wait_ge(s_norm[n], u)
                link(nc.gpsimd.tensor_scalar(spread[n][:, :], moments[n][:, :, 1], eps, None, ALU.add))
                link(nc.gpsimd.tensor_tensor(rstd[n][:, :], spread[n][:, :], minus_half[:, :], ALU.pow))
                link(nc.gpsimd.tensor_tensor(shift[n][:, :], moments[n][:, :, 0], rstd[n][:, :], ALU.mult))
                nc.gpsimd.tensor_scalar(shift[n][:, :], shift[n][:, :], -1.0, None, ALU.mult).then_inc(s_rstd[n], 1)

            def split_up(pair):
                hi, lo = (up_hi0, up_lo0) if pair < 8 else (up_hi1, up_lo1)
                e = slice(2 * pair % 16, 2 * pair % 16 + 2)
                pool.wait_ge(s_hi, pair + 1)
                wait_up(pool, pair)
                nc.gpsimd.tensor_tensor(lo[:, e, :, :], up_raw[:, e, :, :], hi[:, e, :, :].bitcast(fp32),
                                        ALU.subtract).then_inc(s_split, 1)

            def scans(u, k):
                if k == 0:
                    make_rstd("a", u, EPS_C)
                elif k == 9:
                    pool.wait_ge(s_scan_w, u + 1)
                    if u:
                        pool.wait_ge(s_gturn, u)
                    nc.gpsimd.tensor_tensor(square(gated[:, :]), by_image(body(fwd_w)), by_image(body(rev_w)),
                                            ALU.add).then_inc(s_sum_w, 1)
                elif k == 10:
                    pool.wait_ge(s_scan_h, u + 1)
                    link(nc.gpsimd.tensor_tensor(body(fwd_h), body(fwd_h), body(rev_h), ALU.add))
                    pool.wait_ge(s_sum_w, u + 1)
                    nc.gpsimd.tensor_tensor(square(gated[:, :]), square(gated[:, :]), turned(body(fwd_h)),
                                            ALU.add).then_inc(s_sum_h, 1)

            def conv(u, k):
                if k == 1:
                    make_rstd("b", u, SCALE * SCALE * EPS_T)

            def entry(u, k):
                if k == 0:
                    make_rstd("e", u, EPS_T)

            def add_pair(u, i):
                q = pairs_before(u) + i
                if i == 0:
                    return
                pool.wait_ge(s_pm, q + 1)
                if i > 1:
                    pool.wait_ge(s_sum, adds_before(u) + i - 1)
                t = total[:, u % 2, :]
                nc.gpsimd.tensor_tensor(t, t, weighted[:, q % 2, :], ALU.add).then_inc(s_sum, 1)

            def stages(slot):
                for part, u, k in slot:
                    if part == "A":
                        scans(u, k)
                    elif part == "B":
                        conv(u, k)
                    elif part == "E":
                        entry(u, k)

            pair = 0
            for j, slot in enumerate(before):
                stages(slot)
                if j >= 2 and j % 2 == 0 and pair < 8:
                    split_up(pair)
                    pair += 1
            while pair < 8:
                split_up(pair)
                pair += 1
            for u in range(UNITS):
                for i, slot in each_slot(u):
                    if i % 2 == 0:
                        if i >= 4:
                            add_pair(u, i // 2 - 2)
                        elif u:
                            add_pair(u - 1, PAIRS[layer(u - 1)] + i // 2 - 2)
                    stages(slot)
                    if u == 1 and i % 4 == 3:
                        split_up(pair)
                        pair += 1
            for i in (-2, -1):
                add_pair(UNITS - 1, PAIRS[1] + i)

        @block.scalar
        def _(act):
            def load_conv(l):
                s = s_small[l]
                for k in range(2):
                    act.dma_start(in_raw[k * D:(k + 1) * D, l, :], conv_in_w[l]).then_inc(s, 16)
                for k in range(2):
                    part = slice(k * D, (k + 1) * D)
                    act.dma_start(out_raw[part, l, :], conv_out_w[l]).then_inc(s, 16)
                    act.dma_start(gate_raw[part, l, 0:EXPERTS[l]], gate_w[l]).then_inc(s, 16)

            def load_vectors(l):
                at = 0
                for src in (conv_in_b[l], gamma[l], beta[l], conv_out_b[l], gate_b[l]):
                    n = src.shape[0]
                    act.dma_start(vectors[l:l + 1, at:at + n], src.rearrange("(a n) -> a n", a=1)).then_inc(s_vectors, 16)
                    at += n

            act.wait_ge(s_zeroed, 1)
            load_vectors(0)
            load_vectors(1)
            for l in range(LAYERS):
                load_conv(l)

            def round_up(pair):
                hi = up_hi0 if pair < 8 else up_hi1
                e = slice(2 * pair % 16, 2 * pair % 16 + 2)
                wait_up(act, pair)
                nc.scalar.activation(hi[:, e, :, :], up_raw[:, e, :, :], ACT.Copy).then_inc(s_hi, 1)

            def normalise(n, u, src):
                act.wait_ge(s_rstd[n], u + 1)
                if u:
                    act.wait_ge(s_parts[n], u)
                for t in range(TILES):
                    last = nc.scalar.activation(norm[n][:, t, :], src[:, t, :], ACT.Identity,
                                                bias=shift[n][:, t:t + 1], scale=rstd[n][:, t:t + 1])
                last.then_inc(s_norm[n], 1)

            def scans(u, k):
                l = layer(u)
                if k == 2:
                    normalise("a", u, group_rows(u))
                elif k == 4:
                    act.wait_ge(s_turn["a"], u + 1)
                    if u:
                        act.wait_ge(s_proj, 3 * u)
                    nc.scalar.activation(conv_z[:, :], MA[:, :], ACT.Copy).then_inc(s_z["a"], 1)
                elif k == 5:
                    act.wait_ge(s_proj, 3 * u + 1)
                    if u:
                        act.wait_ge(s_add_w, u)
                        act.wait_ge(s_lam, 2 * u)
                    else:
                        act.wait_ge(s_columns, 1)
                    nc.scalar.activation(tanh_f[:, :], MA[:, :], ACT.Tanh, bias=half_bias[:, F_B, l:l + 1],
                                         scale=0.5).then_inc(s_tanh_f, 1)
                elif k == 6:
                    act.wait_ge(s_proj, 3 * u + 2)
                    if u:
                        act.wait_ge(s_add_w, u)
                    nc.scalar.activation(tanh_i[:, :], MA[:, :], ACT.Tanh, bias=half_bias[:, I_B, l:l + 1], scale=0.5)
                    nc.scalar.activation(value_i[:, :], MA[:, :], ACT.Identity,
                                         bias=column(l, I_B)).then_inc(s_value, 1)
                elif k == 7:
                    act.wait_ge(s_tanh_f, u + 1)
                    if u:
                        act.wait_ge(s_scan_w, u)
                        act.wait_ge(s_gated, u)
                    else:
                        act.wait_ge(s_pads, 1)
                    nc.scalar.activation(by_image(body(lam_w)), square(tanh_f[:, :]), ACT.Copy, bias=0.5,
                                         scale=0.5).then_inc(s_lam, 1)
                    act.wait_ge(s_proj, 3 * u + 3)
                    nc.scalar.activation(tanh_o[:, :], MA[:, :], ACT.Tanh, bias=half_bias[:, O_B, l:l + 1],
                                         scale=0.5).then_inc(s_tanh_o, 1)
                elif k == 8:
                    act.wait_ge(s_add_w, u + 1)
                    if u:
                        act.wait_ge(s_scan_h, u)
                    nc.scalar.activation(turned(body(add_h)), by_image(body(add_w)), ACT.Copy).then_inc(s_add_h, 1)
                    nc.scalar.activation(turned(body(lam_h)), square(tanh_f[:, :]), ACT.Copy, bias=0.5,
                                         scale=0.5).then_inc(s_lam, 1)

            def conv(u, k):
                l = layer(u)
                if k == 3:
                    normalise("b", u, heads)
                elif k == 5:
                    act.wait_ge(s_turn["b"], u + 1)
                    if u:
                        act.wait_ge(s_y, u)
                    nc.scalar.activation(heads_z[:, :], MB[:, :], ACT.Copy).then_inc(s_z["b"], 1)
                elif k == 6:
                    act.wait_ge(s_y, u + 1)
                    if u:
                        act.wait_ge(s_yturn, u)
                    else:
                        act.wait_ge(s_outb_ready, LAYERS)
                    nc.scalar.activation(conv_y[:, :], MB[0:D, :], ACT.Identity,
                                         bias=out_bias[:, l:l + 1]).then_inc(s_yc, 1)

            def entry(u, k):
                l = layer(u)
                e = EXPERTS[l]
                if k == 2:
                    normalise("e", u, group_rows(u))
                elif k == 4:
                    act.wait_ge(s_turn["e"], u + 1)
                    if u >= 2:
                        act.wait_ge(s_upb, steps_before(u - 1))
                    nc.scalar.activation(tok_z[:, u % 2, :], ME[:, :], ACT.Copy).then_inc(s_z["e"], 1)
                elif k == 5:
                    act.wait_ge(s_lg, u + 1)
                    if u:
                        act.wait_ge(s_lgturn, u)
                    nc.scalar.activation(logits_t[0:e, :], ME[0:e, :], ACT.Identity,
                                         bias=column(l, GATE_B, e)).then_inc(s_lgc, 1)
                elif k == 8:
                    act.wait_ge(s_margin, u + 1)
                    if u:
                        act.wait_ge(s_gates, u)
                    nc.scalar.activation(tanh_m[:, :], margin[:, :], ACT.Tanh, scale=0.5).then_inc(s_tm, 1)
                elif k == 10:
                    act.wait_ge(s_gateturn, u + 1)
                    if u:
                        act.wait_ge(s_gsent[(u - 1) % 2], 16 * ((u - 1) // 2 + 1))
                    nc.scalar.activation(gates_t[0:e, :], ME[0:e, :], ACT.Copy).then_inc(s_gatec, 1)

            def step(u, i):
                n = steps_before(u) + i
                a = 2 * (n % 2)
                act.wait_ge(s_upa, n + 1)
                if layer(u) == 0:
                    if n >= 2:
                        act.wait_ge(s_hid0, n - 1)
                    nc.scalar.activation(silu_h[:, n % 2, :], UP[:, a, :], ACT.Silu).then_inc(s_silu_h, 1)
                else:
                    if n == N0:
                        act.wait_ge(s_expert_bias, 1)
                    act.wait_ge(s_dn, (n - 4) // 2 + 1)
                    nc.scalar.activation(hidden[:, n % 4, 0, :], UP[:, a, :], ACT.Gelu,
                                         bias=expert_bias[:, 2 * i:2 * i + 1])
                    act.wait_ge(s_upb, n + 1)
                    nc.scalar.activation(hidden[:, n % 4, 1, :], UP[:, a + 1, :], ACT.Gelu,
                                         bias=expert_bias[:, 2 * i + 1:2 * i + 2]).then_inc(s_hid1, 1)

            def stages(slot):
                for part, u, k in slot:
                    if part == "A":
                        scans(u, k)
                    elif part == "B":
                        conv(u, k)
                    elif part == "E":
                        entry(u, k)

            pair = 0
            for j, slot in enumerate(before):
                stages(slot)
                if j >= 2 and j % 2 == 0 and pair < 8:
                    round_up(pair)
                    pair += 1
            while pair < 8:
                round_up(pair)
                pair += 1
            for u in range(UNITS):
                for i, slot in each_slot(u):
                    step(u, i)
                    stages(slot)
                    if u == 1 and i % 4 == 3:
                        round_up(pair)
                        pair += 1

        @block.vector
        def _(dve):
            chain = [0]

            def link(ins):
                chain[0] += 1
                ins.then_inc(s_dve, 1)
                dve.wait_ge(s_dve, chain[0])

            def make_columns():
                dve.wait_ge(s_vectors, 16 * 5 * LAYERS)
                dve.wait_ge(s_zeroed, 2)
                for e in range(2):
                    nc.vector.tensor_copy(wide[:, F_B, e:P:2], vectors[:, 2 * D:3 * D])
                    nc.vector.tensor_copy(wide[:, O_B, e:P:2], vectors[:, D:2 * D])
                    nc.vector.tensor_copy(wide[:, I_B, :].rearrange("p (h d e) -> p h d e", d=2, e=2)[:, :, e, :],
                                          vectors[:, 0:D].rearrange("p (h e) -> p h e", e=2))
                    for which in (GAMMA, BETA, OUT_B):
                        nc.vector.tensor_copy(wide[:, which, e * D:(e + 1) * D], vectors[:, which * D:(which + 1) * D])
                nc.vector.tensor_copy(wide[:, GATE_B, 0:16], vectors[:, 6 * D:6 * D + 16]).then_inc(s_wide, 1)
                dve.wait_ge(s_vturn, 1)
                turned_vectors = DOWN[:, 0:7 * LAYERS].rearrange("p (w l) -> p w l", l=LAYERS)
                nc.vector.tensor_copy(columns[:, :, :], turned_vectors)
                nc.vector.tensor_scalar(half_bias[:, :, :], turned_vectors[:, 0:3, :], 0.5, None,
                                        ALU.mult).then_inc(s_columns, 1)

            def conv_weights(l):
                dve.wait_ge(s_small[l], 16 * 6)
                dve.wait_ge(s_columns, 1)
                fog = in_wide
                for e in range(2):
                    nc.vector.tensor_copy(fog[:, FORGET, e:P:2], in_raw[:, l, 2 * D:3 * D])
                    nc.vector.tensor_copy(fog[:, OUTPUT, e:P:2], in_raw[:, l, D:2 * D])
                    d = e
                    nc.vector.tensor_copy(
                        fog[:, INPUT, :].rearrange("p (h d e) -> p h d e", d=2, e=2)[:, :, d, :],
                        in_raw[:, l, 0:D].rearrange("p (h e) -> p h e", e=2))
                link(nc.vector.tensor_scalar(out_scaled[:, l, :], out_raw[:, l, :], column(l, GAMMA), -1.0,
                                             ALU.mult, ALU.mult))
                e = EXPERTS[l]
                nc.vector.tensor_copy(in_hi[:, l, :, :], fog[:, :, :])
                nc.vector.tensor_copy(out_hi[:, l, :], out_scaled[:, l, :])
                link(nc.vector.tensor_copy(gate_hi[:, l, 0:e], gate_raw[:, l, 0:e]))
                nc.vector.tensor_tensor(in_lo[:, l, :, :], fog[:, :, :], in_hi[:, l, :, :].bitcast(fp32), ALU.subtract)
                nc.vector.tensor_tensor(out_lo[:, l, :], out_scaled[:, l, :], out_hi[:, l, :].bitcast(fp32), ALU.subtract)
                nc.vector.tensor_tensor(gate_lo[:, l, 0:e], gate_raw[:, l, 0:e], gate_hi[:, l, 0:e].bitcast(fp32),
                                        ALU.subtract).then_inc(s_conv_w, 1)

            def biases_ready():
                dve.wait_ge(s_outb, 1)
                dve.wait_ge(s_columns, 1)
                for l in range(LAYERS):
                    nc.vector.tensor_tensor(out_bias[:, l:l + 1], DOWN[0:D, l:l + 1], column(l, OUT_B, D),
                                            ALU.add).then_inc(s_outb_ready, 1)
                nc.vector.tensor_copy(expert_bias[:, :], DOWN[:, 32:52]).then_inc(s_expert_bias, 1)

            def make_moments(n, u, src):
                if u:
                    dve.wait_ge(s_rstd[n], u)
                for t in range(TILES):
                    last = nc.vector.bn_stats(stats[n][:, t, :], src[:, t, :])
                link(last)
                for t in range(TILES):
                    last = nc.vector.bn_aggr(moments[n][:, t, :], stats[n][:, t, :])
                last.then_inc(s_stats[n], 1)

            def make_parts(n, u):
                dve.wait_ge(s_norm[n], u + 1)
                if u:
                    dve.wait_ge(s_turn[n], u)
                link(nc.vector.tensor_copy(parts[n][:, :, 0, :].bitcast(fp32r), norm[n][:, :, :]))
                nc.vector.tensor_tensor(parts[n][:, :, 1, :], norm[n][:, :, :], parts[n][:, :, 0, :],
                                        ALU.subtract).then_inc(s_parts[n], 1)

            def scans(u, k):
                if k == 0:
                    if u < GROUPS:
                        dve.wait_ge(s_x[min(u, 1)], 16 * HALF)
                    else:
                        dve.wait_ge(s_exit, u - GROUPS + 1)
                    make_moments("a", u, group_rows(u))
                elif k == 3:
                    make_parts("a", u)
                elif k == 7:
                    dve.wait_ge(s_value, u + 1)
                    link(nc.vector.scalar_tensor_tensor(value_i[:, :], tanh_i[:, :], 1.0, value_i[:, :],
                                                        ALU.add, ALU.mult))
                    if u:
                        dve.wait_ge(s_add_h, u)
                        dve.wait_ge(s_scan_w, u)
                    else:
                        dve.wait_ge(s_pads, 1)
                    dve.wait_ge(s_tanh_f, u + 1)
                    nc.vector.scalar_tensor_tensor(by_image(body(add_w)), square(tanh_f[:, :]), 1.0,
                                                   square(value_i[:, :]), ALU.subtract, ALU.mult).then_inc(s_add_w, 1)
                elif k == 8:
                    dve.wait_ge(s_add_w, u + 1)
                    dve.wait_ge(s_lam, 2 * u + 1)
                    if u:
                        dve.wait_ge(s_sum_w, u)
                    nc.vector.tensor_tensor_scan(fwd_w[:, 0:SCAN - 1], lam_w[:, 0:SCAN - 1], add_w[:, 0:SCAN - 1],
                                                 0.0, ALU.mult, ALU.add)
                    nc.vector.tensor_tensor_scan(rev_w[:, SCAN - 1:0:-1], lam_w[:, SCAN - 1:0:-1],
                                                 add_w[:, SCAN - 1:0:-1], 0.0, ALU.mult, ALU.add).then_inc(s_scan_w, 1)
                elif k == 9:
                    dve.wait_ge(s_add_h, u + 1)
                    dve.wait_ge(s_lam, 2 * u + 2)
                    if u:
                        dve.wait_ge(s_sum_h, u)
                    nc.vector.tensor_tensor_scan(fwd_h[:, 0:SCAN - 1], lam_h[:, 0:SCAN - 1], add_h[:, 0:SCAN - 1],
                                                 0.0, ALU.mult, ALU.add)
                    nc.vector.tensor_tensor_scan(rev_h[:, SCAN - 1:0:-1], lam_h[:, SCAN - 1:0:-1],
                                                 add_h[:, SCAN - 1:0:-1], 0.0, ALU.mult, ALU.add).then_inc(s_scan_h, 1)
                elif k == 11:
                    dve.wait_ge(s_sum_h, u + 1)
                    dve.wait_ge(s_tanh_o, u + 1)
                    nc.vector.scalar_tensor_tensor(gated[:, :], tanh_o[:, :], 1.0, gated[:, :],
                                                   ALU.add, ALU.mult).then_inc(s_gated, 1)

            def conv(u, k):
                if k == 1:
                    dve.wait_ge(s_gturn, u + 1)
                    if u:
                        dve.wait_ge(s_norm["b"], u)
                    link(nc.vector.tensor_reduce(
                        heads[:, :, :].rearrange("p t (h e) -> p (t h) e", e=2),
                        MB[:, :].rearrange("p (t h d e) -> p (t h) e d", t=TILES, d=2, e=2),
                        mybir.AxisListType.X, ALU.add))
                    make_moments("b", u, heads)
                elif k == 4:
                    make_parts("b", u)
                elif k == 8:
                    dve.wait_ge(s_yturn, u + 1)
                    r = group_rows(u)
                    nc.vector.tensor_tensor(r, r, MB[:, 0:TILES * D].rearrange("p (t d) -> p t d", t=TILES),
                                            ALU.add).then_inc(s_conv, 1)

            def entry(u, k):
                l = layer(u)
                e = EXPERTS[l]
                if k == 0:
                    dve.wait_ge(s_conv, u + 1)
                    make_moments("e", u, group_rows(u))
                elif k == 3:
                    make_parts("e", u)
                elif k == 7:
                    dve.wait_ge(s_lgturn, u + 1)
                    if u == 0:
                        dve.wait_ge(s_const, 2)
                        nc.vector.tensor_copy(iota[:, :], iota_i[:, :])
                    link(nc.vector.tensor_copy(logits[:, :, 0:e], ME[:, 0:TILES * e].rearrange("p (t e) -> p t e", t=TILES)))
                    for t in range(TILES):
                        last = nc.vector.max(best[:, t, :], logits[:, t, 0:e])
                    link(last)
                    nc.vector.tensor_tensor(margin[:, :], best[:, :, 0], best[:, :, 1], ALU.subtract).then_inc(s_margin, 1)
                    for t in range(TILES):
                        last = nc.vector.max_index(best_at[:, t, :], best[:, t, :], logits[:, t, 0:e])
                    link(last)
                    link(nc.vector.tensor_copy(best_atf[:, :, :], best_at[:, :, 0:2]))
                    for k2 in range(2):
                        last = nc.vector.tensor_tensor(
                            pick[:, k2, :, 0:e], iota[:, 0:e].unsqueeze(1).broadcast_to([P, TILES, e]),
                            best_atf[:, :, k2:k2 + 1].broadcast_to([P, TILES, e]), ALU.is_equal)
                    last.then_inc(s_lgread, 1)
                elif k == 9:
                    dve.wait_ge(s_tm, u + 1)
                    nc.vector.tensor_scalar(shares[:, :, 0], tanh_m[:, :], 0.5, 0.5, ALU.mult, ALU.add)
                    link(nc.vector.tensor_scalar(shares[:, :, 1], tanh_m[:, :], -0.5, 0.5, ALU.mult, ALU.add))
                    dve.wait_ge(s_lgread, u + 1)
                    for k2 in range(2):
                        last = nc.vector.tensor_tensor(pick[:, k2, :, 0:e], pick[:, k2, :, 0:e],
                                                       shares[:, :, k2:k2 + 1].broadcast_to([P, TILES, e]), ALU.mult)
                    link(last)
                    if u:
                        dve.wait_ge(s_gateturn, u)
                    nc.vector.tensor_tensor(gates[:, :, 0:e], pick[:, 0, :, 0:e], pick[:, 1, :, 0:e],
                                            ALU.add).then_inc(s_gates, 1)

            def leave(u, k):
                if k == 1:
                    dve.wait_ge(s_xturn, u + 1)
                    dve.wait_ge(s_conv, u + 1)
                    r = group_rows(u)
                    m = tiles(ME[:, :])
                    link(nc.vector.tensor_tensor(r, r, m[:, :, 0:D], ALU.add))
                    nc.vector.tensor_tensor(r, r, m[:, :, D:P], ALU.add).then_inc(s_exit, 1)

            def step(u, i):
                if layer(u):
                    return
                n = steps_before(u) + i
                dve.wait_ge(s_silu_h, n + 1)
                dve.wait_ge(s_upb, n + 1)
                if n >= 4:
                    dve.wait_ge(s_dn, (n - 4) // 2 + 1)
                nc.vector.tensor_tensor(hidden[:, n % 4, 0, :], silu_h[:, n % 2, :], UP[:, 2 * (n % 2) + 1, :],
                                        ALU.mult).then_inc(s_hid0, 1)

            def weigh_pair(u, i):
                q = pairs_before(u) + i
                dve.wait_ge(s_dn, q + 1)
                g = gates_b[:, u % 2, i, :]
                if i == 0:
                    dve.wait_ge(s_gback[u % 2], 32 * (u // 2 + 1))
                    if u >= 2:
                        dve.wait_ge(s_xturn, u - 1)
                    dst = total[:, u % 2, :]
                else:
                    dst = weighted[:, q % 2, :]
                    if i > 2:
                        dve.wait_ge(s_sum, adds_before(u) + i - 2)
                    elif u:
                        dve.wait_ge(s_sum, adds_before(u))
                if layer(u) == 0:
                    nc.vector.tensor_tensor(dst, DOWN[:, :], g, ALU.mult).then_inc(s_pm, 1)
                else:
                    nc.vector.scalar_tensor_tensor(dst, DOWN[:, :], expert_bias[:, 16 + i:17 + i], g,
                                                   ALU.add, ALU.mult).then_inc(s_pm, 1)

            def stages(slot):
                for part, u, k in slot:
                    if part == "A":
                        scans(u, k)
                    elif part == "B":
                        conv(u, k)
                    elif part == "E":
                        entry(u, k)
                    else:
                        leave(u, k)

            for j, slot in enumerate(before):
                stages(slot)
                if j == 2:
                    make_columns()
                    conv_weights(0)
                elif j == A_STAGES:
                    biases_ready()
                elif j == BEFORE - 2:
                    conv_weights(1)
            for u in range(UNITS):
                for i, slot in each_slot(u):
                    step(u, i)
                    if i % 2 == 0:
                        if i >= 4:
                            weigh_pair(u, i // 2 - 2)
                        elif u:
                            weigh_pair(u - 1, PAIRS[layer(u - 1)] + i // 2 - 2)
                    stages(slot)
            for i in (-2, -1):
                weigh_pair(UNITS - 1, PAIRS[1] + i)
            leave(UNITS - 1, 1)

        @block.tensor
        def _(pe):
            def product(dst, hi, lo, z):
                nc.tensor.matmul(dst, hi, z, start=True, stop=False)
                return nc.tensor.matmul(dst, lo, z, start=False, stop=True)

            def turn(dst, src, k=P):
                return nc.tensor.transpose(dst, src, ident[0:k, 0:k])

            def turn_vectors():
                pe.wait_ge(s_wide, 1)
                for which in range(7):
                    last = turn(DOWN[:, which * LAYERS:(which + 1) * LAYERS], wide[:, which, :], LAYERS)
                last.then_inc(s_vturn, 1)

            def small_products():
                pe.wait_ge(s_columns, 1)
                pe.wait_ge(s_expert_rows, 32)
                for l in range(LAYERS):
                    pe.wait_ge(s_small[l], 16 * 6)
                    nc.tensor.matmul(DOWN[0:D, l:l + 1], out_raw[0:D, l, :], column(l, BETA, D), start=True, stop=True)
                turn(DOWN[:, 32:52], expert_rows[:, :], 20).then_inc(s_outb, 1)

            def turn_parts(n, u, dst):
                pe.wait_ge(s_parts[n], u + 1)
                for t in range(TILES):
                    last = turn(dst[:, t * P:(t + 1) * P], parts[n][:, t, :, :].rearrange("p k d -> p (k d)"))
                last.then_inc(s_turn[n], 1)

            def wait_me(part, u):
                if me_before[part, u]:
                    was, v = me_before[part, u]
                    pe.wait_ge(s_gatec if was == "E" else s_exit, v + 1)

            def scans(u, k):
                l = layer(u)
                if k == 4:
                    if u:
                        pe.wait_ge(s_tanh_o, u)
                    turn_parts("a", u, MA)
                elif k == 5:
                    pe.wait_ge(s_z["a"], u + 1)
                    if u in (0, GROUPS):
                        pe.wait_ge(s_conv_w, l + 1)
                    product(MA[:, :], in_hi[:, l, FORGET, :], in_lo[:, l, FORGET, :], conv_z[:, :]).then_inc(s_proj, 1)
                elif k == 6:
                    pe.wait_ge(s_tanh_f, u + 1)
                    product(MA[:, :], in_hi[:, l, INPUT, :], in_lo[:, l, INPUT, :], conv_z[:, :]).then_inc(s_proj, 1)
                elif k == 7:
                    pe.wait_ge(s_value, u + 1)
                    product(MA[:, :], in_hi[:, l, OUTPUT, :], in_lo[:, l, OUTPUT, :], conv_z[:, :]).then_inc(s_proj, 1)

            def conv(u, k):
                l = layer(u)
                if k == 0:
                    pe.wait_ge(s_gated, u + 1)
                    if u:
                        pe.wait_ge(s_conv, u)
                    for t in range(TILES):
                        last = turn(MB[:, t * P:(t + 1) * P], gated[:, t * P:(t + 1) * P])
                    last.then_inc(s_gturn, 1)
                elif k == 5:
                    pe.wait_ge(s_stats["b"], u + 1)
                    turn_parts("b", u, MB)
                elif k == 6:
                    pe.wait_ge(s_z["b"], u + 1)
                    product(MB[0:D, :], out_hi[:, l, :], out_lo[:, l, :], heads_z[:, :]).then_inc(s_y, 1)
                elif k == 7:
                    pe.wait_ge(s_yc, u + 1)
                    for t in range(TILES):
                        last = turn(MB[:, t * D:(t + 1) * D], conv_y[:, t * P:(t + 1) * P], D)
                    last.then_inc(s_yturn, 1)

            def entry(u, k):
                l = layer(u)
                e = EXPERTS[l]
                if k == 4:
                    wait_me("E", u)
                    turn_parts("e", u, ME)
                elif k == 5:
                    pe.wait_ge(s_z["e"], u + 1)
                    product(ME[0:e, :], gate_hi[:, l, 0:e], gate_lo[:, l, 0:e], tok_z[:, u % 2, :]).then_inc(s_lg, 1)
                elif k == 6:
                    pe.wait_ge(s_lgc, u + 1)
                    for t in range(TILES):
                        last = turn(ME[:, t * e:(t + 1) * e], logits_t[0:e, t * P:(t + 1) * P], e)
                    last.then_inc(s_lgturn, 1)
                elif k == 10:
                    pe.wait_ge(s_gates, u + 1)
                    for t in range(TILES):
                        last = turn(ME[0:e, t * P:(t + 1) * P], gates[:, t, 0:e])
                    last.then_inc(s_gateturn, 1)

            def leave(u, k):
                if k == 0:
                    pe.wait_ge(s_sum, adds_before(u + 1))
                    wait_me("X", u)
                    for t in range(TILES):
                        last = turn(ME[:, t * P:(t + 1) * P], total[:, u % 2, t * P:(t + 1) * P])
                    last.then_inc(s_xturn, 1)

            def up(u, i):
                n = steps_before(u) + i
                a = 2 * (n % 2)
                if i == 0:
                    pe.wait_ge(s_z["e"], u + 1)
                if n >= 2:
                    wait_hidden(pe, n - 2)
                if i % 2 == 0 and u in (0, GROUPS):
                    pe.wait_ge(s_split, 8 * layer(u) + i // 2 + 1)
                hi, lo = (up_hi1, up_lo1) if layer(u) else (up_hi0, up_lo0)
                z = tok_z[:, u % 2, :]
                product(UP[:, a, :], hi[:, i, 0, :], lo[:, i, 0, :], z).then_inc(s_upa, 1)
                product(UP[:, a + 1, :], hi[:, i, 1, :], lo[:, i, 1, :], z).then_inc(s_upb, 1)

            def down(u, i):
                q = pairs_before(u) + i
                wait_hidden(pe, 2 * q + 1)
                if q:
                    pe.wait_ge(s_pm, q)
                else:
                    pe.wait_ge(s_expert_bias, 1)
                if i == 0 and u in (0, GROUPS):
                    pe.wait_ge(s_down[layer(u)], 16)
                chunks = 1 + layer(u)
                for j in range(chunks):
                    for k in range(2):
                        w = down1[:, 2 * i + k, j, :] if layer(u) else down0[:, 2 * i + k, :]
                        last = nc.tensor.matmul(DOWN[k * D:(k + 1) * D, :], w, hidden[:, (2 * q + k) % 4, j, :],
                                                start=(j == 0), stop=(j == chunks - 1))
                last.then_inc(s_dn, 1)

            def stages(slot):
                for part, u, k in slot:
                    if part == "A":
                        scans(u, k)
                    elif part == "B":
                        conv(u, k)
                    elif part == "E":
                        entry(u, k)
                    else:
                        leave(u, k)

            pe.wait_ge(s_const, 1)
            for j, slot in enumerate(before):
                if j == 3:
                    turn_vectors()
                elif j == A_STAGES:
                    small_products()
                stages(slot)
            for u in range(UNITS):
                for i, slot in each_slot(u):
                    up(u, i)
                    if i % 2:
                        if i >= LAG:
                            down(u, (i - LAG) // 2)
                        elif u:
                            down(u - 1, PAIRS[layer(u - 1)] - 1)
                    stages(slot)
            down(UNITS - 1, PAIRS[1] - 1)
            leave(UNITS - 1, 0)


_INS = ['x', 'L0_conv_in_w', 'L0_conv_in_b', 'L0_conv_out_w', 'L0_conv_out_b', 'L0_conv_gamma', 'L0_conv_beta',
        'L0_ffn_gate_w', 'L0_ffn_gate_b', 'L0_ffn_w1', 'L0_ffn_w2', 'L0_ffn_w3',
        'L1_conv_in_w', 'L1_conv_in_b', 'L1_conv_out_w', 'L1_conv_out_b', 'L1_conv_gamma', 'L1_conv_beta',
        'L1_ffn_Wg', 'L1_ffn_bg', 'L1_ffn_W1', 'L1_ffn_b1', 'L1_ffn_W2', 'L1_ffn_b2']


def kernel(**inputs):
    import numpy as _np
    import concourse.bacc as _bacc
    from concourse import mybir as _mybir
    from concourse.bass_utils import run_bass_kernel_spmd as _run

    nc = _bacc.Bacc("TRN2", target_bir_lowering=False, num_devices=1)
    arrays, args = {}, []
    for name in _INS:
        a = _np.ascontiguousarray(inputs[name])
        arrays[f"in_{name}_dram"] = a
        args.append(nc.dram_tensor(f"in_{name}_dram", a.shape, _mybir.dt.from_np(a.dtype), kind="ExternalInput").ap())
    args.append(nc.dram_tensor("out_dram", (H, W, B, D), _mybir.dt.float32, kind="ExternalOutput").ap())
    metaformer(nc, *args)
    r = _run(nc, [arrays], core_ids=[0])
    return r.results[0]["out_dram"]
```

```python
import concourse.bass as bass
from concourse import mybir
from contextlib import ExitStack

H, W, B, D = 16, 16, 8, 64
P = 128
GB = 2
GROUPS = B // GB
LAYERS = 2
UNITS = LAYERS * GROUPS
TOK = GB * H * W
HALF = H * W // P
TILES = GB * HALF
SEQ = 16
NSEQ = TOK // SEQ
PAD = SEQ + 1
SCAN = NSEQ * PAD + 1
EXPERTS = (16, 8)
STEPS = EXPERTS
PAIRS = tuple(e // 2 for e in EXPERTS)
HID = 128
EPS_C = 1e-6
EPS_T = 1e-5
SCALE = -8.0
SUMS_BY_VECTOR = 4
NORM_BY_SCALAR = {"a": (4, 7), "b": (3, 4), "e": (0, 2)}
LAG = 3


def layer(u):
    return u // GROUPS


def by_scalar(n, u):
    first, last = NORM_BY_SCALAR[n]
    return first <= u <= last


def by_scalar_up_to(n, u):
    return sum(by_scalar(n, v) for v in range(u + 1))


def steps_before(u):
    return sum(STEPS[layer(v)] for v in range(u))


def pairs_before(u):
    return steps_before(u) // 2


def adds_before(u):
    return pairs_before(u) - u


UP_CHUNKS = ((0, 0, 4), (0, 4, 16), (1, 0, 8))


SLOTS = 16
GAPS = ({"A": (1, 3, 2, 1, 1, 1, 2, 1, 2, 1, 3),
         "B": (1, 3, 3, 1, 1, 2),
         "E": (1, 2, 1, 1, 1, 1, 1, 1, 3),
         "X": (1, 1)},
        {"A": (1, 3, 2, 1, 1, 1, 2, 2, 2, 2, 1),
         "B": (1, 2, 2, 1, 3, 1),
         "E": (1, 4, 1, 1, 2, 1, 1, 1, 1),
         "X": (1, 1)})
FIRST_GAP = 1
A_PERIOD = 5
SECOND_FROM = 1
A_FROM = (-2, -2, -2, -2, -5, -2, -2, 1)
FIRST_GATES = 2
X_FROM = 6
ME_FROM = 3
BEFORE = 21
BIASES_AT = 12
SPLIT_FROM, SPLIT_STEP, SPLIT_LEAD = 18, 3, 4


def chunk(pair):
    l, e = pair // PAIRS[0], 2 * (pair % PAIRS[0])
    return next(c for c, (layer_, first, end) in enumerate(UP_CHUNKS) if layer_ == l and first <= e < end)


def schedule():
    slots = [(-1, j) for j in range(BEFORE)] + [(u, j) for u in range(UNITS) for j in range(SLOTS)]
    plan, me_before, me_last = {}, {}, None
    done = {p: [0] * UNITS for p in "ABEX"}
    at = {p: [-99] * UNITS for p in "ABEX"}

    def complete(p, v):
        return done[p][v] == len(GAPS[0][p])

    def current(p):
        return next((v for v in range(UNITS) if not complete(p, v)), UNITS)

    for n, (u, j) in enumerate(slots):
        here = []

        def go(p, v):
            nonlocal me_last
            if (p == "X" and not done[p][v]) or (p == "E" and done[p][v] == ME_FROM):
                me_before[p, v], me_last = me_last, (p, v)
            here.append((p, v, done[p][v]))
            done[p][v] += 1
            at[p][v] = n

        def may(p, v, after):
            if complete(p, v):
                return False
            if not done[p][v]:
                return all(complete(q, w) and at[q][w] < n for q, w in after)
            return n - at[p][v] >= (GAPS[layer(u)][p][done[p][v]] if u >= 0 else FIRST_GAP if v else 1)

        x, e = current("X"), current("E")
        if x < u and may("X", x, ()) and (done["X"][x] or (j >= X_FROM or x < u - 1)
                                          and (e == UNITS or done["E"][e] <= ME_FROM)):
            go("X", x)
        elif e < UNITS and e <= u + 1:
            due = len(GAPS[0]["E"]) if e == u and j == 2 else ME_FROM + 1 if e == u + 1 and last_slot(u, j) else 0
            while may("E", e, [("B", e)]) or done["E"][e] < due:
                if done["E"][e] == ME_FROM and 0 < (done["X"][x] if x < UNITS else 0) < len(GAPS[0]["X"]):
                    break
                go("E", e)
                if done["E"][e] >= due:
                    break
        b = current("B")
        if b < UNITS and may("B", b, [("A", b)]):
            go("B", b)
        for v in range(UNITS):
            if v and not done["A"][v] and (done["A"][v - 1] < A_PERIOD or
                                           (done["A"][v - 1] == A_PERIOD and at["A"][v - 1] == n)):
                break
            if v and not done["A"][v] and n < max(SECOND_FROM, BEFORE + SLOTS * (v - 3) + A_FROM[v]):
                break
            if may("A", v, [("X", v - GROUPS)] if v >= GROUPS else []):
                go("A", v)
        plan[u, j] = sorted(here, key=lambda s: ("XEBA".index(s[0]), s[1:]))
        assert not last_slot(u, j) or done["E"][u + 1] > ME_FROM, (u, done)
        assert u < 0 or j != 2 or complete("E", u), (u, done)
    me_before["X", UNITS - 1] = me_last
    assert current("A") == current("B") == current("E") == UNITS and current("X") == UNITS - 1
    return ([plan[-1, j] for j in range(BEFORE)], [[plan[u, j] for j in range(SLOTS)] for u in range(UNITS)],
            me_before)


def pairs_split_at(n):
    return [p for p in range(PAIRS[0]) if n == min(SPLIT_FROM + SPLIT_STEP * p, BEFORE + 2 * p - SPLIT_LEAD)]


def last_slot(u, j):
    return u + 1 < UNITS and j == (SLOTS if u >= 0 else BEFORE) - 1


def metaformer(nc, x, L0_conv_in_w, L0_conv_in_b, L0_conv_out_w, L0_conv_out_b, L0_conv_gamma, L0_conv_beta,
               L0_ffn_gate_w, L0_ffn_gate_b, L0_ffn_w1, L0_ffn_w2, L0_ffn_w3,
               L1_conv_in_w, L1_conv_in_b, L1_conv_out_w, L1_conv_out_b, L1_conv_gamma, L1_conv_beta,
               L1_ffn_Wg, L1_ffn_bg, L1_ffn_W1, L1_ffn_b1, L1_ffn_W2, L1_ffn_b2, out):
    fp32, fp32r = mybir.dt.float32, mybir.dt.float32r
    i32, u32 = mybir.dt.int32, mybir.dt.uint32
    ALU = mybir.AluOpType
    ACT = mybir.ActivationFunctionType

    conv_in_w, conv_in_b = (L0_conv_in_w, L1_conv_in_w), (L0_conv_in_b, L1_conv_in_b)
    conv_out_w, conv_out_b = (L0_conv_out_w, L1_conv_out_w), (L0_conv_out_b, L1_conv_out_b)
    gamma, beta = (L0_conv_gamma, L1_conv_gamma), (L0_conv_beta, L1_conv_beta)
    gate_w, gate_b = (L0_ffn_gate_w, L1_ffn_Wg), (L0_ffn_gate_b, L1_ffn_bg)
    x_rows = x.rearrange("(f h) w b d -> (h w) f (b d)", f=HALF)
    out_rows = out.rearrange("(f h) w b d -> (h w) f (b d)", f=HALF)

    before, beside, me_before = schedule()

    ctx = ExitStack()
    with ctx:
        def sb(name, shape, dt=fp32):
            return ctx.enter_context(nc.sbuf_tensor(name, shape, dt))

        def sem(name):
            return ctx.enter_context(nc.semaphore(name))

        ident = sb("ident", [P, P])
        iota_i = sb("iota_i", [P, 16], i32)
        iota = sb("iota", [P, 16])
        over_d = sb("over_d", [P, D])
        minus_half = sb("minus_half", [P, TILES])
        rows = sb("rows", [P, HALF, GROUPS, GB, D])
        in_raw = sb("in_raw", [P, LAYERS, 3 * D])
        in_wide = sb("in_wide", [P, 3, P])
        in_hi = sb("in_hi", [P, LAYERS, 3, P], fp32r)
        in_lo = sb("in_lo", [P, LAYERS, 3, P], fp32r)
        out_raw = sb("out_raw", [D, LAYERS, D])
        out_scaled = sb("out_scaled", [D + 1, LAYERS, D])
        gate_raw = sb("gate_raw", [P, LAYERS, 16])
        vectors = sb("vectors", [LAYERS, 6 * D + 16])
        wide = sb("wide", [LAYERS, 5, P])
        columns = sb("columns", [P, 5, LAYERS])
        half_bias = sb("half_bias", [P, 3, LAYERS])
        expert_rows = sb("expert_rows", [20, P])
        expert_bias = sb("expert_bias", [P, 20])
        gate_bias = sb("gate_bias", [P, LAYERS, 16])
        up_raw = sb("up_raw", [P, 16, 2, HID])
        up_hi0 = sb("up_hi0", [P, 16, 2, HID], fp32r)
        up_lo0 = sb("up_lo0", [P, 16, 2, HID], fp32r)
        up_hi1 = sb("up_hi1", [P, 8, 2, HID], fp32r)
        up_lo1 = sb("up_lo1", [P, 8, 2, HID], fp32r)
        down0 = sb("down0", [P, 16, D])
        down1 = sb("down1", [P, 8, 2, D])
        stats = {n: sb(f"stats_{n}", [P, TILES, 6]) for n in "abe"}
        moments = {n: sb(f"moments_{n}", [P, TILES, 2]) for n in "abe"}
        spread = {n: sb(f"spread_{n}", [P, TILES]) for n in "abe"}
        rstd = {n: sb(f"rstd_{n}", [P, TILES]) for n in "abe"}
        shift = {n: sb(f"shift_{n}", [P, TILES]) for n in "abe"}
        norm = {n: sb(f"norm_{n}", [P, TILES, D]) for n in "abe"}
        parts = {n: sb(f"parts_{n}", [P, TILES, 2, D]) for n in "ae"}
        conv_z = sb("conv_z", [P, TOK], fp32r)
        tanh_f = sb("tanh_f", [P, TOK])
        tanh_i = sb("tanh_i", [P, TOK])
        tanh_o = sb("tanh_o", [P, TOK])
        value_i = sb("value_i", [P, TOK])
        lam_w = sb("lam_w", [P, SCAN])
        lam_h = sb("lam_h", [P, SCAN])
        add_w = sb("add_w", [P, SCAN])
        add_h = sb("add_h", [P, SCAN])
        fwd_w, rev_w, fwd_h, rev_h = (sb(n, [P, SCAN]) for n in ("fwd_w", "rev_w", "fwd_h", "rev_h"))
        gated = sb("gated", [P, TOK])
        heads_z = sb("heads_z", [D + 1, TOK])
        tok_z = sb("tok_z", [P, 2, TOK], fp32r)
        logits = sb("logits", [P, TILES, 16])
        best = sb("best", [P, TILES, 8])
        best_at = sb("best_at", [P, TILES, 8], u32)
        best_atf = sb("best_atf", [P, TILES, 2])
        margin = sb("margin", [P, TILES])
        tanh_m = sb("tanh_m", [P, TILES])
        shares = sb("shares", [P, TILES, 2])
        pick = sb("pick", [P, 2, TILES, 16])
        gates = sb("gates", [P, TILES, 16])
        gates_t = sb("gates_t", [16, TOK])
        gates_b = sb("gates_b", [P, 2, 8, TOK])
        silu_h = sb("silu_h", [P, 2, TOK])
        hidden = sb("hidden", [P, 4, 2, TOK])
        weighted = sb("weighted", [P, 2, TOK])
        total = sb("total", [P, 2, TOK])

        gates_dram = nc.dram_tensor("gates_dram", (UNITS, 16, TOK), fp32, kind="Internal").ap()

        UP = ctx.enter_context(nc.psum_tensor("UP", [P, 4, TOK], fp32))
        DOWN = ctx.enter_context(nc.psum_tensor("DOWN", [P, TOK], fp32))
        MA, MB, ME = (ctx.enter_context(nc.psum_tensor(n, [P, TOK], fp32)) for n in ("MA", "MB", "ME"))

        heads = MB[:, 0:TILES * D].rearrange("p (i f d) -> p i f d", i=GB, f=HALF)

        F_B, O_B, I_B, GAMMA, BETA = range(5)

        def column(l, which, n=P):
            return columns[0:n, which, l:l + 1]

        FORGET, INPUT, OUTPUT = range(3)
        GATE_AT, EXPERT_AT = LAYERS * D, LAYERS * (D + 16)

        def tiles(t):
            return t.rearrange("p (t n) -> p t n", t=TILES)

        def body(t):
            return t[:, 0:NSEQ * PAD].rearrange("p (s n) -> p s n", n=PAD)[:, :, 1:PAD]

        def by_image(ap):
            return ap.rearrange("p (i s) n -> p i s n", i=GB)

        def turned(ap):
            return ap.rearrange("p (i s) n -> p i n s", i=GB)

        def square(t):
            return t.rearrange("p (i s n) -> p i s n", i=GB, s=H)

        s_x = [sem("rows_loaded_first"), sem("rows_loaded_others")]
        s_small = [sem(f"conv_weights_loaded{l}") for l in range(LAYERS)]
        s_up = [sem(f"up_loaded{c}") for c in range(len(UP_CHUNKS))]
        s_down = [sem(f"down_loaded{l}") for l in range(LAYERS)]
        s_in = [sem(f"in_weights_loaded{l}") for l in range(LAYERS)]
        s_in_b = sem("in_biases_loaded")
        s_vectors = sem("vectors_loaded")
        s_expert_rows = sem("expert_rows_loaded")
        s_ones = sem("row_of_ones_ready")
        s_zeroed = sem("vector_rows_zeroed")
        s_const = sem("constants_ready")
        s_pads = sem("pads_zeroed")
        s_wide = sem("vectors_widened")
        s_bias_products = sem("bias_products")
        s_biases = sem("biases_ready")
        s_conv_w = sem("in_weights_split")
        s_out_w = sem("out_weights_ready")
        s_hi = sem("up_high_parts")
        s_split = sem("up_pairs_split")
        s_vturn = sem("vectors_turned")
        s_columns = sem("columns_ready")
        s_dve = sem("vector_chain")
        s_pool = sem("pool_chain")
        s_stats = {n: sem(f"moments_ready_{n}") for n in "abe"}
        s_rstd = {n: sem(f"rstd_ready_{n}") for n in "abe"}
        s_high = {n: sem(f"high_parts_by_scalar_{n}") for n in "abe"}
        s_norm = {n: sem(f"normalised_{n}") for n in "abe"}
        s_parts = {n: sem(f"norm_parts_ready_{n}") for n in "abe"}
        s_turn = {n: sem(f"norm_turned_{n}") for n in "abe"}
        s_z = {n: sem(f"norm_columns_ready_{n}") for n in "abe"}
        s_proj = sem("projections_done")
        s_tanh_f = sem("tanh_f_ready")
        s_value = sem("value_i_ready")
        s_tanh_o = sem("tanh_o_ready")
        s_lam = sem("lambdas_ready")
        s_add_w = sem("row_inputs_ready")
        s_add_h = sem("column_inputs_ready")
        s_scan_w = sem("row_scans_done")
        s_scan_h = sem("column_scans_done")
        s_sum_w = sem("row_scans_summed")
        s_sum_h = sem("column_scans_summed")
        s_gated = sem("gated_ready")
        s_gturn = sem("gated_turned")
        s_heads = sem("heads_ready")
        s_y = sem("conv_output_product")
        s_conv = sem("conv_residual_done")
        s_lg = sem("logits_product")
        s_margin = sem("margin_ready")
        s_pick = sem("best_marked")
        s_tm = sem("margin_tanh")
        s_gates = sem("gates_ready")
        s_gateturn = sem("gates_turned")
        s_gatec = sem("gates_copied")
        s_gsent = [sem(f"gates_sent{k}") for k in range(2)]
        s_gfirst = sem("first_gates_broadcast")
        s_gback = [sem(f"gates_broadcast{k}") for k in range(2)]
        s_upa = sem("up_first_bank")
        s_upb = sem("up_second_bank")
        s_silu_h = sem("silu_ready")
        s_hid0 = sem("hidden_ready0")
        s_hid1a = sem("hidden_first_half_ready1")
        s_hid1 = sem("hidden_ready1")
        s_dn = sem("pair_down_done")
        s_pm = sem("pair_weighted")
        s_sum = sem("pair_added")
        s_xturn = sem("total_turned")
        s_exit = sem("exit_residual_done")
        s_out = sem("rows_stored")

        N0 = steps_before(GROUPS)

        def wait_hidden(eng, n):
            if n < N0:
                eng.wait_ge(s_hid0, n + 1)
            else:
                eng.wait_ge(s_hid1, n + 1 - N0)

        def each_slot(u):
            per = SLOTS // STEPS[layer(u)]
            for i in range(STEPS[layer(u)]):
                yield i, [s for j in range(per) for s in beside[u][per * i + j]]

        def group_rows(u):
            return rows[:, :, u % GROUPS, :, :].rearrange("p f i d -> p i f d")

        def by_tile(t):
            return t.rearrange("p (i f) d -> p i f d", i=GB)

        def wait_up(eng, pair):
            eng.wait_ge(s_up[chunk(pair)], 64 if pair < PAIRS[0] else 32)

        block = ctx.enter_context(nc.Block())

        @block.sync
        def _(sp):
            def load_rows(first, end, s):
                sp.dma_start(rows[:, :, first:end, :, :].rearrange("p f g i d -> p f (g i d)"),
                             x_rows[:, :, first * GB * D:end * GB * D]).then_inc(s, 16)

            def load_up(c):
                l, first, end = UP_CHUNKS[c]
                e = slice(first, end)
                for k in range(2):
                    part = slice(k * D, (k + 1) * D)
                    if l == 0:
                        for n, w in enumerate((L0_ffn_w1, L0_ffn_w2)):
                            sp.dma_start(up_raw[part, e, n, :], w[e, :, :].rearrange("e d h -> d e h")).then_inc(s_up[c], 16)
                    else:
                        sp.dma_start(up_raw[part, e, :, :],
                                     L1_ffn_W1[e, :, :].rearrange("e d (j h) -> d e j h", j=2)).then_inc(s_up[c], 16)

            def load_vector(l, at, src, s):
                sp.dma_start(vectors[l:l + 1, at:at + src.shape[0]], src.rearrange("(a n) -> a n", a=1)).then_inc(s, 16)

            def load_in(l):
                for k in range(2):
                    sp.dma_start(in_raw[k * D:(k + 1) * D, l, :], conv_in_w[l]).then_inc(s_in[l], 16)

            def load_conv(l):
                sp.dma_start(out_raw[:, l, :], conv_out_w[l]).then_inc(s_small[l], 16)
                for k in range(2):
                    sp.dma_start(gate_raw[k * D:(k + 1) * D, l, 0:EXPERTS[l]], gate_w[l]).then_inc(s_small[l], 16)

            load_rows(0, 1, s_x[0])
            load_in(0)
            sp.wait_ge(s_zeroed, 1)
            for l in range(LAYERS):
                load_vector(l, 0, conv_in_b[l], s_in_b)
            for l in range(LAYERS):
                for i, src in enumerate((gamma[l], beta[l], conv_out_b[l], gate_b[l])):
                    load_vector(l, (3 + i) * D, src, s_vectors)
            load_rows(1, GROUPS, s_x[1])
            load_conv(0)
            load_up(0)
            load_conv(1)
            load_up(1)
            sp.dma_start(expert_rows[0:16, :], L1_ffn_b1.rearrange("e (j h) -> (e j) h", j=2)).then_inc(s_expert_rows, 16)
            sp.dma_start(expert_rows[16:20, :], L1_ffn_b2.rearrange("(q k) o -> q (k o)", k=2)).then_inc(s_expert_rows, 16)
            sp.dma_start(down0[:, :, :], L0_ffn_w3.rearrange("e h o -> h e o")).then_inc(s_down[0], 16)
            load_in(1)
            sp.dma_start(down1[:, :, :, :], L1_ffn_W2.rearrange("e (j h) o -> h e j o", j=2)).then_inc(s_down[1], 16)

            def load_up1():
                sp.wait_ge(s_split, PAIRS[0])
                load_up(2)

            def broadcast_gates(u):
                sp.wait_ge(s_gatec, u + 1)
                e = EXPERTS[layer(u)]
                sp.dma_start(gates_dram[u, 0:e, :], gates_t[0:e, :]).then_inc(s_gsent[u % 2], 16)
                sp.wait_ge(s_gsent[u % 2], 16 * (u // 2 + 1))
                if u >= 2:
                    sp.wait_ge(s_pm, pairs_before(u - 1))
                by_pair = gates_dram[u, 0:e, :].rearrange("(q k) n -> k q n", k=2)
                loads = ((0, FIRST_GATES, s_gfirst), (FIRST_GATES, e // 2, s_gback[0])) if u == 0 else ((0, e // 2, s_gback[u % 2]),)
                for first, end, s in loads:
                    for k in range(2):
                        sp.dma_start(gates_b[k * D:(k + 1) * D, u % 2, first:end, :],
                                     by_pair[k:k + 1, first:end, :].broadcast_to([D, end - first, TOK])).then_inc(s, 16)

            def store_rows(u):
                g = u % GROUPS
                sp.wait_ge(s_exit, u + 1)
                sp.dma_start(out_rows[:, :, g * GB * D:(g + 1) * GB * D],
                             rows[:, :, g, :, :].rearrange("p f i d -> p f (i d)")).then_inc(s_out, 16)

            for u in range(UNITS):
                broadcast_gates(u)
                if u == 0:
                    load_up1()
                if u >= GROUPS + 2:
                    store_rows(u - 2)
            for u in (UNITS - 2, UNITS - 1):
                store_rows(u)
            sp.wait_ge(s_out, 16 * GROUPS)

        @block.gpsimd
        def _(pool):
            chain = [0]

            def link(ins):
                chain[0] += 1
                ins.then_inc(s_pool, 1)
                pool.wait_ge(s_pool, chain[0])

            nc.gpsimd.memset(vectors[:, :], 0.0).then_inc(s_zeroed, 1)
            link(nc.gpsimd.memset(ident[:, :], 0.0))
            nc.gpsimd.affine_select(out=ident[:, :], in_=ident[:, :], compare_op=ALU.not_equal, fill=1.0, base=0,
                                    pattern=[[-1, P]], channel_multiplier=1).then_inc(s_const, 1)
            link(nc.gpsimd.iota(iota_i[:, :], [[1, 16]], base=0, channel_multiplier=0))
            pool.wait_ge(s_const, 1)
            by_channel = ident[:, :].rearrange("p (h d e) -> p h d e", d=2, e=2)
            nc.gpsimd.tensor_tensor(over_d[:, :].rearrange("p (h e) -> p h e", e=2), by_channel[:, :, 0, :],
                                    by_channel[:, :, 1, :], ALU.add).then_inc(s_const, 1)
            nc.gpsimd.tensor_copy(iota[:, :], iota_i[:, :]).then_inc(s_const, 1)
            link(nc.gpsimd.memset(minus_half[:, :], -0.5))
            for t in (lam_w, lam_h, add_w, add_h):
                last = nc.gpsimd.memset(t[:, 0:SCAN:PAD], 0.0)
            last.then_inc(s_pads, 1)

            def make_rstd(n, u, eps):
                pool.wait_ge(s_stats[n], u + 1)
                if u:
                    pool.wait_ge(s_turn[n], u)
                link(nc.gpsimd.tensor_scalar(spread[n][:, :], moments[n][:, :, 1], eps, None, ALU.add))
                last = nc.gpsimd.tensor_tensor(rstd[n][:, :], spread[n][:, :], minus_half[:, :], ALU.pow)
                if by_scalar(n, u):
                    link(last)
                    link(nc.gpsimd.tensor_tensor(shift[n][:, :], moments[n][:, :, 0], rstd[n][:, :], ALU.mult))
                    last = nc.gpsimd.tensor_scalar(shift[n][:, :], shift[n][:, :], -1.0, None, ALU.mult)
                last.then_inc(s_rstd[n], 1)

            def split_up(pair):
                hi, lo = (up_hi0, up_lo0) if pair < 8 else (up_hi1, up_lo1)
                e = slice(2 * pair % 16, 2 * pair % 16 + 2)
                pool.wait_ge(s_hi, pair + 1)
                wait_up(pool, pair)
                nc.gpsimd.tensor_tensor(lo[:, e, :, :], up_raw[:, e, :, :], hi[:, e, :, :].bitcast(fp32),
                                        ALU.subtract).then_inc(s_split, 1)

            def scans(u, k):
                if k == 0:
                    make_rstd("a", u, EPS_C)
                elif k == 8:
                    pool.wait_ge(s_scan_w, u + 1)
                    if u:
                        pool.wait_ge(s_gturn, u)
                    nc.gpsimd.tensor_tensor(square(gated[:, :]), by_image(body(fwd_w)), by_image(body(rev_w)),
                                            ALU.add).then_inc(s_sum_w, 1)
                elif k == 9 and u >= SUMS_BY_VECTOR:
                    pool.wait_ge(s_scan_h, u + 1)
                    link(nc.gpsimd.tensor_tensor(body(fwd_h), body(fwd_h), body(rev_h), ALU.add))
                    pool.wait_ge(s_sum_w, u + 1)
                    nc.gpsimd.tensor_tensor(square(gated[:, :]), square(gated[:, :]), turned(body(fwd_h)),
                                            ALU.add).then_inc(s_sum_h, 1)

            def conv(u, k):
                if k == 0:
                    make_rstd("b", u, SCALE * SCALE * EPS_T)

            def entry(u, k):
                e = EXPERTS[layer(u)]
                if k == 0:
                    make_rstd("e", u, EPS_T)
                elif k == 7:
                    pool.wait_ge(s_tm, u + 1)
                    nc.gpsimd.tensor_scalar(shares[:, :, 0], tanh_m[:, :], 0.5, 0.5, ALU.mult, ALU.add)
                    link(nc.gpsimd.tensor_scalar(shares[:, :, 1], tanh_m[:, :], -0.5, 0.5, ALU.mult, ALU.add))
                    pool.wait_ge(s_pick, u + 1)
                    p, share = pick[:, :, :, 0:e], shares[:, :, :].rearrange("p t k -> p k t").unsqueeze(3)
                    link(nc.gpsimd.tensor_tensor(p, p, share.broadcast_to([P, 2, TILES, e]), ALU.mult))
                    if u:
                        pool.wait_ge(s_gateturn, u)
                    nc.gpsimd.tensor_tensor(gates[:, :, 0:e], pick[:, 0, :, 0:e], pick[:, 1, :, 0:e],
                                            ALU.add).then_inc(s_gates, 1)

            def add_pair(u, i):
                q = pairs_before(u) + i
                if i == 0:
                    return
                pool.wait_ge(s_pm, q + 1)
                if i > 1:
                    pool.wait_ge(s_sum, adds_before(u) + i - 1)
                t = total[:, u % 2, :]
                nc.gpsimd.tensor_tensor(t, t, weighted[:, q % 2, :], ALU.add).then_inc(s_sum, 1)

            def stages(slot):
                for part, u, k in slot:
                    if part == "A":
                        scans(u, k)
                    elif part == "B":
                        conv(u, k)
                    elif part == "E":
                        entry(u, k)

            for j, slot in enumerate(before):
                stages(slot)
                for pair in pairs_split_at(j):
                    split_up(pair)
            for u in range(UNITS):
                for i, slot in each_slot(u):
                    if i % 2 == 0:
                        if i >= 4:
                            add_pair(u, i // 2 - 2)
                        elif u:
                            add_pair(u - 1, PAIRS[layer(u - 1)] + i // 2 - 2)
                    stages(slot)
                    if u == 0:
                        for pair in pairs_split_at(BEFORE + i):
                            split_up(pair)
                    if u == 1 and i % 4 == 3:
                        split_up(PAIRS[0] + i // 4)
            for i in (-2, -1):
                add_pair(UNITS - 1, PAIRS[1] + i)

        @block.scalar
        def _(act):
            def round_up(pair):
                hi = up_hi0 if pair < 8 else up_hi1
                e = slice(2 * pair % 16, 2 * pair % 16 + 2)
                wait_up(act, pair)
                nc.scalar.activation(hi[:, e, :, :], up_raw[:, e, :, :], ACT.Copy).then_inc(s_hi, 1)

            def normalise(n, u, tile):
                if not by_scalar(n, u):
                    return
                act.wait_ge(s_rstd[n], u + 1)
                if u:
                    act.wait_ge(s_turn[n], u)
                for t in range(TILES):
                    last = nc.scalar.activation(norm[n][:, t, :], tile[:, t // HALF, t % HALF, :], ACT.Identity,
                                                bias=shift[n][:, t:t + 1], scale=rstd[n][:, t:t + 1])
                last.then_inc(s_norm[n], 1)
                if n == "b":
                    return
                act.wait_ge(s_norm[n], u + 1)
                nc.scalar.activation(parts[n][:, :, 0, :].bitcast(fp32r), norm[n][:, :, :],
                                     ACT.Copy).then_inc(s_high[n], 1)

            def scans(u, k):
                l = layer(u)
                if k == 1:
                    normalise("a", u, group_rows(u))
                elif k == 3:
                    act.wait_ge(s_turn["a"], u + 1)
                    if u:
                        act.wait_ge(s_proj, 3 * u)
                    nc.scalar.activation(conv_z[:, :], MA[:, :], ACT.Copy).then_inc(s_z["a"], 1)
                elif k == 4:
                    act.wait_ge(s_proj, 3 * u + 1)
                    if u:
                        act.wait_ge(s_add_w, u)
                        act.wait_ge(s_lam, 2 * u)
                    else:
                        act.wait_ge(s_columns, 1)
                    nc.scalar.activation(tanh_f[:, :], MA[:, :], ACT.Tanh, bias=half_bias[:, F_B, l:l + 1],
                                         scale=0.5).then_inc(s_tanh_f, 1)
                elif k == 5:
                    act.wait_ge(s_proj, 3 * u + 2)
                    if u:
                        act.wait_ge(s_add_w, u)
                    nc.scalar.activation(tanh_i[:, :], MA[:, :], ACT.Tanh, bias=half_bias[:, I_B, l:l + 1], scale=0.5)
                    nc.scalar.activation(value_i[:, :], MA[:, :], ACT.Identity,
                                         bias=column(l, I_B)).then_inc(s_value, 1)
                elif k == 6:
                    act.wait_ge(s_tanh_f, u + 1)
                    if u:
                        act.wait_ge(s_scan_w, u)
                        act.wait_ge(s_gated, u)
                    else:
                        act.wait_ge(s_pads, 1)
                    nc.scalar.activation(by_image(body(lam_w)), square(tanh_f[:, :]), ACT.Copy, bias=0.5,
                                         scale=0.5).then_inc(s_lam, 1)
                    act.wait_ge(s_proj, 3 * u + 3)
                    nc.scalar.activation(tanh_o[:, :], MA[:, :], ACT.Tanh, bias=half_bias[:, O_B, l:l + 1],
                                         scale=0.5).then_inc(s_tanh_o, 1)
                elif k == 7:
                    act.wait_ge(s_add_w, u + 1)
                    if u:
                        act.wait_ge(s_scan_h, u)
                    nc.scalar.activation(turned(body(add_h)), by_image(body(add_w)), ACT.Copy).then_inc(s_add_h, 1)
                    nc.scalar.activation(turned(body(lam_h)), square(tanh_f[:, :]), ACT.Copy, bias=0.5,
                                         scale=0.5).then_inc(s_lam, 1)

            def conv(u, k):
                l = layer(u)
                if k == 1:
                    normalise("b", u, heads)
                elif k == 3:
                    act.wait_ge(s_turn["b"], u + 1)
                    if u:
                        act.wait_ge(s_y, u)
                    nc.scalar.activation(heads_z[0:D, :], MB[0:D, :], ACT.Copy).then_inc(s_z["b"], 1)

            def entry(u, k):
                l = layer(u)
                e = EXPERTS[l]
                if k == 1:
                    normalise("e", u, group_rows(u))
                elif k == 3:
                    act.wait_ge(s_turn["e"], u + 1)
                    if u >= 2:
                        act.wait_ge(s_upb, steps_before(u - 1))
                    nc.scalar.activation(tok_z[:, u % 2, :], ME[:, :], ACT.Copy).then_inc(s_z["e"], 1)
                elif k == 6:
                    act.wait_ge(s_margin, u + 1)
                    if u:
                        act.wait_ge(s_gates, u)
                    nc.scalar.activation(tanh_m[:, :], margin[:, :], ACT.Tanh, scale=0.5).then_inc(s_tm, 1)
                elif k == 8:
                    act.wait_ge(s_gateturn, u + 1)
                    if u:
                        act.wait_ge(s_gsent[(u - 1) % 2], 16 * ((u - 1) // 2 + 1))
                    nc.scalar.activation(gates_t[0:e, :], ME[0:e, :], ACT.Copy).then_inc(s_gatec, 1)

            def step(u, i):
                n = steps_before(u) + i
                a = 2 * (n % 2)
                act.wait_ge(s_upa, n + 1)
                if layer(u) == 0:
                    if n >= 2:
                        act.wait_ge(s_hid0, n - 1)
                    nc.scalar.activation(silu_h[:, n % 2, :], UP[:, a, :], ACT.Silu).then_inc(s_silu_h, 1)
                else:
                    if n == N0:
                        act.wait_ge(s_biases, 1)
                    act.wait_ge(s_dn, (n - 4) // 2 + 1)
                    nc.scalar.activation(hidden[:, n % 4, 0, :], UP[:, a, :], ACT.Gelu,
                                         bias=expert_bias[:, 2 * i:2 * i + 1]).then_inc(s_hid1a, 1)
                    act.wait_ge(s_upb, n + 1)
                    nc.scalar.activation(hidden[:, n % 4, 1, :], UP[:, a + 1, :], ACT.Gelu,
                                         bias=expert_bias[:, 2 * i + 1:2 * i + 2]).then_inc(s_hid1, 1)

            def stages(slot):
                for part, u, k in slot:
                    if part == "A":
                        scans(u, k)
                    elif part == "B":
                        conv(u, k)
                    elif part == "E":
                        entry(u, k)

            for j, slot in enumerate(before):
                stages(slot)
                for pair in pairs_split_at(j):
                    round_up(pair)
            for u in range(UNITS):
                for i, slot in each_slot(u):
                    step(u, i)
                    stages(slot)
                    if u == 0:
                        for pair in pairs_split_at(BEFORE + i):
                            round_up(pair)
                    if u == 1 and i % 4 == 3:
                        round_up(PAIRS[0] + i // 4)

        @block.vector
        def _(dve):
            chain = [0]

            def link(ins):
                chain[0] += 1
                ins.then_inc(s_dve, 1)
                dve.wait_ge(s_dve, chain[0])

            def turned_vectors(first, end):
                return DOWN[:, first * LAYERS:end * LAYERS].rearrange("p (w l) -> p w l", l=LAYERS)

            def widen_in_biases():
                dve.wait_ge(s_in_b, 16 * LAYERS)
                for e in range(2):
                    nc.vector.tensor_copy(wide[:, F_B, e:P:2], vectors[:, 2 * D:3 * D])
                    nc.vector.tensor_copy(wide[:, O_B, e:P:2], vectors[:, D:2 * D])
                    last = nc.vector.tensor_copy(
                        wide[:, I_B, :].rearrange("p (h d e) -> p h d e", d=2, e=2)[:, :, e, :],
                        vectors[:, 0:D].rearrange("p (h e) -> p h e", e=2))
                last.then_inc(s_wide, 1)

            def in_biases():
                dve.wait_ge(s_vturn, 1)
                nc.vector.tensor_copy(columns[:, 0:3, :], turned_vectors(0, 3))
                nc.vector.tensor_scalar(half_bias[:, :, :], turned_vectors(0, 3), 0.5, None,
                                        ALU.mult).then_inc(s_columns, 1)

            def widen_vectors():
                dve.wait_ge(s_vectors, 16 * 4 * LAYERS)
                both = wide[:, GAMMA:BETA + 1, :].rearrange("p w (k d) -> p w k d", k=2)
                once = vectors[:, 3 * D:5 * D].rearrange("p (w d) -> p w d", d=D)
                for k in range(2):
                    last = nc.vector.tensor_copy(both[:, :, k, :], once)
                last.then_inc(s_wide, 1)

            def vectors_ready():
                dve.wait_ge(s_vturn, 2)
                nc.vector.tensor_copy(columns[:, 3:5, :], turned_vectors(3, 5)).then_inc(s_columns, 1)

            def in_weights(l):
                dve.wait_ge(s_in[l], 32)
                fog = in_wide
                for e in range(2):
                    nc.vector.tensor_copy(fog[:, FORGET, e:P:2], in_raw[:, l, 2 * D:3 * D])
                    nc.vector.tensor_copy(fog[:, OUTPUT, e:P:2], in_raw[:, l, D:2 * D])
                    d = e
                    last = nc.vector.tensor_copy(
                        fog[:, INPUT, :].rearrange("p (h d e) -> p h d e", d=2, e=2)[:, :, d, :],
                        in_raw[:, l, 0:D].rearrange("p (h e) -> p h e", e=2))
                link(last)
                link(nc.vector.tensor_copy(in_hi[:, l, :, :], fog[:, :, :]))
                nc.vector.tensor_tensor(in_lo[:, l, :, :], fog[:, :, :], in_hi[:, l, :, :].bitcast(fp32),
                                        ALU.subtract).then_inc(s_conv_w, 1)

            def out_weights(l):
                dve.wait_ge(s_small[l], 16 * 3)
                dve.wait_ge(s_columns, 2)
                nc.vector.tensor_scalar(out_scaled[0:D, l, :], out_raw[:, l, :], column(l, GAMMA, D), -1.0,
                                        ALU.mult, ALU.mult).then_inc(s_out_w, 1)

            def biases_ready():
                dve.wait_ge(s_bias_products, 1)
                nc.vector.tensor_copy(out_scaled[D:D + 1, :, :],
                                      DOWN[D:D + 1, 0:LAYERS * D].rearrange("p (l d) -> p l d", d=D))
                nc.vector.tensor_copy(gate_bias[:, :, :],
                                      DOWN[:, GATE_AT:GATE_AT + 16 * LAYERS].rearrange("p (l e) -> p l e", e=16))
                nc.vector.tensor_copy(expert_bias[:, :], DOWN[:, EXPERT_AT:EXPERT_AT + 20]).then_inc(s_biases, 1)

            def make_moments(n, u, tile):
                if u:
                    dve.wait_ge(s_rstd[n], u)
                for t in range(TILES):
                    last = nc.vector.bn_stats(stats[n][:, t, :], tile[:, t // HALF, t % HALF, :])
                link(last)
                for t in range(TILES):
                    last = nc.vector.bn_aggr(moments[n][:, t, :], stats[n][:, t, :])
                last.then_inc(s_stats[n], 1)
                if not by_scalar(n, u):
                    dve.wait_ge(s_stats[n], u + 1)
                    if u:
                        dve.wait_ge(s_turn[n], u)
                    mean = moments[n][:, :, 0:1].broadcast_to([P, TILES, D])
                    nc.vector.tensor_tensor(by_tile(norm[n]), tile, by_tile(mean), ALU.subtract).then_inc(s_norm[n], 1)

            def make_parts(n, u):
                if n == "b":
                    if not by_scalar(n, u):
                        dve.wait_ge(s_rstd[n], u + 1)
                        dve.wait_ge(s_norm[n], u + 1)
                        nc.vector.tensor_tensor(norm[n][:, :, :], norm[n][:, :, :],
                                                rstd[n][:, :].unsqueeze(2).broadcast_to([P, TILES, D]),
                                                ALU.mult).then_inc(s_parts[n], 1)
                    return
                high, low = parts[n][:, :, 0, :], parts[n][:, :, 1, :]
                if by_scalar(n, u):
                    dve.wait_ge(s_high[n], by_scalar_up_to(n, u))
                else:
                    dve.wait_ge(s_rstd[n], u + 1)
                    dve.wait_ge(s_norm[n], u + 1)
                    link(nc.vector.tensor_tensor(norm[n][:, :, :], norm[n][:, :, :],
                                                 rstd[n][:, :].unsqueeze(2).broadcast_to([P, TILES, D]), ALU.mult))
                    link(nc.vector.tensor_copy(high.bitcast(fp32r), norm[n][:, :, :]))
                nc.vector.tensor_tensor(low, norm[n][:, :, :], high, ALU.subtract).then_inc(s_parts[n], 1)

            def scans(u, k):
                if k == 0:
                    if u < GROUPS:
                        dve.wait_ge(s_x[min(u, 1)], 16)
                    else:
                        dve.wait_ge(s_exit, u - GROUPS + 1)
                    make_moments("a", u, group_rows(u))
                elif k == 2:
                    make_parts("a", u)
                elif k == 6:
                    dve.wait_ge(s_value, u + 1)
                    link(nc.vector.scalar_tensor_tensor(value_i[:, :], tanh_i[:, :], 1.0, value_i[:, :],
                                                        ALU.add, ALU.mult))
                    if u:
                        dve.wait_ge(s_add_h, u)
                        dve.wait_ge(s_scan_w, u)
                    else:
                        dve.wait_ge(s_pads, 1)
                    dve.wait_ge(s_tanh_f, u + 1)
                    nc.vector.scalar_tensor_tensor(by_image(body(add_w)), square(tanh_f[:, :]), 1.0,
                                                   square(value_i[:, :]), ALU.subtract, ALU.mult).then_inc(s_add_w, 1)
                elif k == 7:
                    dve.wait_ge(s_add_w, u + 1)
                    dve.wait_ge(s_lam, 2 * u + 1)
                    if u:
                        dve.wait_ge(s_sum_w, u)
                    nc.vector.tensor_tensor_scan(fwd_w[:, 0:SCAN - 1], lam_w[:, 0:SCAN - 1], add_w[:, 0:SCAN - 1],
                                                 0.0, ALU.mult, ALU.add)
                    nc.vector.tensor_tensor_scan(rev_w[:, SCAN - 1:0:-1], lam_w[:, SCAN - 1:0:-1],
                                                 add_w[:, SCAN - 1:0:-1], 0.0, ALU.mult, ALU.add).then_inc(s_scan_w, 1)
                elif k == 8:
                    dve.wait_ge(s_add_h, u + 1)
                    dve.wait_ge(s_lam, 2 * u + 2)
                    if u:
                        dve.wait_ge(s_sum_h, u)
                    nc.vector.tensor_tensor_scan(fwd_h[:, 0:SCAN - 1], lam_h[:, 0:SCAN - 1], add_h[:, 0:SCAN - 1],
                                                 0.0, ALU.mult, ALU.add)
                    nc.vector.tensor_tensor_scan(rev_h[:, SCAN - 1:0:-1], lam_h[:, SCAN - 1:0:-1],
                                                 add_h[:, SCAN - 1:0:-1], 0.0, ALU.mult, ALU.add).then_inc(s_scan_h, 1)
                elif k == 9 and u < SUMS_BY_VECTOR:
                    dve.wait_ge(s_scan_h, u + 1)
                    link(nc.vector.tensor_tensor(body(fwd_h), body(fwd_h), body(rev_h), ALU.add))
                    dve.wait_ge(s_sum_w, u + 1)
                    nc.vector.tensor_tensor(square(gated[:, :]), square(gated[:, :]), turned(body(fwd_h)),
                                            ALU.add).then_inc(s_sum_h, 1)
                elif k == 10:
                    dve.wait_ge(s_sum_h, u + 1)
                    dve.wait_ge(s_tanh_o, u + 1)
                    nc.vector.scalar_tensor_tensor(gated[:, :], tanh_o[:, :], 1.0, gated[:, :],
                                                   ALU.add, ALU.mult).then_inc(s_gated, 1)

            def conv(u, k):
                if k == 0:
                    dve.wait_ge(s_gturn, u + 1)
                    make_moments("b", u, heads)
                elif k == 2:
                    make_parts("b", u)
                elif k == 5:
                    dve.wait_ge(s_y, u + 1)
                    r = group_rows(u)
                    nc.vector.tensor_tensor(r, r, by_tile(MB[:, 0:TILES * D].rearrange("p (t d) -> p t d", t=TILES)),
                                            ALU.add).then_inc(s_conv, 1)

            def entry(u, k):
                l = layer(u)
                e = EXPERTS[l]
                if k == 0:
                    dve.wait_ge(s_conv, u + 1)
                    make_moments("e", u, group_rows(u))
                elif k == 2:
                    make_parts("e", u)
                elif k == 5:
                    dve.wait_ge(s_lg, u + 1)
                    if u == 0:
                        dve.wait_ge(s_biases, 1)
                    link(nc.vector.tensor_tensor(
                        logits[:, :, 0:e], ME[:, 0:TILES * e].rearrange("p (t e) -> p t e", t=TILES),
                        gate_bias[:, l, 0:e].unsqueeze(1).broadcast_to([P, TILES, e]), ALU.add))
                    for t in range(TILES):
                        last = nc.vector.max(best[:, t, :], logits[:, t, 0:e])
                    link(last)
                    nc.vector.tensor_tensor(margin[:, :], best[:, :, 0], best[:, :, 1], ALU.subtract).then_inc(s_margin, 1)
                    for t in range(TILES):
                        last = nc.vector.max_index(best_at[:, t, :], best[:, t, :], logits[:, t, 0:e])
                    link(last)
                    link(nc.vector.tensor_copy(best_atf[:, :, :], best_at[:, :, 0:2]))
                    if u:
                        dve.wait_ge(s_gates, u)
                    else:
                        dve.wait_ge(s_const, 3)
                    places = iota[:, 0:e].unsqueeze(1).unsqueeze(1).broadcast_to([P, 2, TILES, e])
                    at = best_atf[:, :, :].rearrange("p t k -> p k t").unsqueeze(3).broadcast_to([P, 2, TILES, e])
                    nc.vector.tensor_tensor(pick[:, :, :, 0:e], places, at, ALU.is_equal).then_inc(s_pick, 1)

            def leave(u, k):
                if k == 1:
                    dve.wait_ge(s_xturn, u + 1)
                    dve.wait_ge(s_conv, u + 1)
                    r = group_rows(u)
                    m = tiles(ME[:, :])
                    link(nc.vector.tensor_tensor(r, r, by_tile(m[:, :, 0:D]), ALU.add))
                    nc.vector.tensor_tensor(r, r, by_tile(m[:, :, D:P]), ALU.add).then_inc(s_exit, 1)

            def step(u, i):
                if layer(u):
                    return
                n = steps_before(u) + i
                dve.wait_ge(s_silu_h, n + 1)
                dve.wait_ge(s_upb, n + 1)
                if n >= 4:
                    dve.wait_ge(s_dn, (n - 4) // 2 + 1)
                nc.vector.tensor_tensor(hidden[:, n % 4, 0, :], silu_h[:, n % 2, :], UP[:, 2 * (n % 2) + 1, :],
                                        ALU.mult).then_inc(s_hid0, 1)

            def weigh_pair(u, i):
                q = pairs_before(u) + i
                dve.wait_ge(s_dn, q + 1)
                g = gates_b[:, u % 2, i, :]
                if u == 0 and i == 0:
                    dve.wait_ge(s_gfirst, 32)
                elif i == (FIRST_GATES if u == 0 else 0):
                    dve.wait_ge(s_gback[u % 2], 32 * (u // 2 + 1))
                if i == 0:
                    if u >= 2:
                        dve.wait_ge(s_xturn, u - 1)
                    dst = total[:, u % 2, :]
                else:
                    dst = weighted[:, q % 2, :]
                    if i > 2:
                        dve.wait_ge(s_sum, adds_before(u) + i - 2)
                    elif u:
                        dve.wait_ge(s_sum, adds_before(u))
                if layer(u) == 0:
                    nc.vector.tensor_tensor(dst, DOWN[:, :], g, ALU.mult).then_inc(s_pm, 1)
                else:
                    nc.vector.scalar_tensor_tensor(dst, DOWN[:, :], expert_bias[:, 16 + i:17 + i], g,
                                                   ALU.add, ALU.mult).then_inc(s_pm, 1)

            def stages(slot):
                for part, u, k in slot:
                    if part == "A":
                        scans(u, k)
                    elif part == "B":
                        conv(u, k)
                    elif part == "E":
                        entry(u, k)
                    else:
                        leave(u, k)

            nc.vector.memset(heads_z[D:D + 1, :], 1.0).then_inc(s_ones, 1)
            def weigh_due_pair(u, i):
                if i % 2 == 0:
                    if i >= 4:
                        weigh_pair(u, i // 2 - 2)
                    elif u:
                        weigh_pair(u - 1, PAIRS[layer(u - 1)] + i // 2 - 2)

            for j, slot in enumerate(before):
                stages(slot)
                if j == 1:
                    in_weights(0)
                elif j == 2:
                    widen_in_biases()
                elif j == 3:
                    in_biases()
                elif j == 4:
                    widen_vectors()
                elif j == 6:
                    vectors_ready()
                    out_weights(0)
                elif j == BIASES_AT + 1:
                    biases_ready()
            for u in range(UNITS):
                for i, slot in each_slot(u):
                    if u == 1 and i == 3:
                        in_weights(1)
                    elif u == 1 and i == 7:
                        out_weights(1)
                    weigh_due_pair(u, i)
                    stages(slot)
                    step(u, i)
            for i in (-2, -1):
                weigh_pair(UNITS - 1, PAIRS[1] + i)
            leave(UNITS - 1, 1)

        @block.tensor
        def _(pe):
            def product(dst, hi, lo, z):
                nc.tensor.matmul(dst, hi, z, start=True, stop=False)
                return nc.tensor.matmul(dst, lo, z, start=False, stop=True)

            def turn(dst, src, k=P):
                return nc.tensor.transpose(dst, src, ident[0:k, 0:k])

            def turn_vectors(first, end, count):
                pe.wait_ge(s_wide, count)
                for which in range(first, end):
                    last = turn(DOWN[:, which * LAYERS:(which + 1) * LAYERS], wide[:, which, :], LAYERS)
                last.then_inc(s_vturn, 1)

            def small_products():
                pe.wait_ge(s_columns, 2)
                pe.wait_ge(s_vectors, 16 * 4 * LAYERS)
                pe.wait_ge(s_expert_rows, 32)
                for l in range(LAYERS):
                    pe.wait_ge(s_small[l], 16 * 3)
                    row = ident[0:LAYERS, l:l + 1].broadcast_to([LAYERS, P])
                    nc.tensor.matmul(DOWN[:, l * D:(l + 1) * D], column(l, BETA, D).broadcast_to([D, P]),
                                     out_raw[:, l, :], start=True, stop=False)
                    nc.tensor.matmul(DOWN[:, l * D:(l + 1) * D], row, vectors[:, 5 * D:6 * D], start=False, stop=True)
                    nc.tensor.matmul(DOWN[:, GATE_AT + 16 * l:GATE_AT + 16 * (l + 1)], row,
                                     vectors[:, 6 * D:6 * D + 16], start=True, stop=True)
                turn(DOWN[:, EXPERT_AT:EXPERT_AT + 20], expert_rows[:, :], 20).then_inc(s_bias_products, 1)

            def turn_parts(n, u, dst):
                pe.wait_ge(s_parts[n], u + 1)
                for t in range(TILES):
                    last = turn(dst[:, t * P:(t + 1) * P], parts[n][:, t, :, :].rearrange("p k d -> p (k d)"))
                last.then_inc(s_turn[n], 1)

            def wait_me(part, u):
                if me_before[part, u]:
                    was, v = me_before[part, u]
                    pe.wait_ge(s_gatec if was == "E" else s_exit, v + 1)

            def scans(u, k):
                l = layer(u)
                if k == 3:
                    if u:
                        pe.wait_ge(s_tanh_o, u)
                    turn_parts("a", u, MA)
                elif k == 4:
                    pe.wait_ge(s_z["a"], u + 1)
                    if u in (0, GROUPS):
                        pe.wait_ge(s_conv_w, l + 1)
                    product(MA[:, :], in_hi[:, l, FORGET, :], in_lo[:, l, FORGET, :], conv_z[:, :]).then_inc(s_proj, 1)
                elif k == 5:
                    pe.wait_ge(s_tanh_f, u + 1)
                    product(MA[:, :], in_hi[:, l, INPUT, :], in_lo[:, l, INPUT, :], conv_z[:, :]).then_inc(s_proj, 1)
                elif k == 6:
                    pe.wait_ge(s_value, u + 1)
                    product(MA[:, :], in_hi[:, l, OUTPUT, :], in_lo[:, l, OUTPUT, :], conv_z[:, :]).then_inc(s_proj, 1)

            def conv(u, k):
                l = layer(u)
                if k == 0:
                    pe.wait_ge(s_gated, u + 1)
                    if u:
                        pe.wait_ge(s_conv, u)
                    else:
                        pe.wait_ge(s_const, 2)
                    for t in range(TILES):
                        last = nc.tensor.matmul(MB[:, t * D:(t + 1) * D], gated[:, t * P:(t + 1) * P], over_d[:, :],
                                                start=True, stop=True)
                    last.then_inc(s_gturn, 1)
                elif k == 3:
                    pe.wait_ge(s_norm["b"], u + 1)
                    if not by_scalar("b", u):
                        pe.wait_ge(s_parts["b"], u + 1 - by_scalar_up_to("b", u))
                    for t in range(TILES):
                        last = turn(MB[0:D, t * P:(t + 1) * P], norm["b"][:, t, :])
                    last.then_inc(s_turn["b"], 1)
                elif k == 4:
                    pe.wait_ge(s_z["b"], u + 1)
                    if u in (0, GROUPS):
                        pe.wait_ge(s_ones, 1)
                        pe.wait_ge(s_out_w, l + 1)
                        pe.wait_ge(s_biases, 1)
                    for t in range(TILES):
                        last = nc.tensor.matmul(MB[:, t * D:(t + 1) * D], heads_z[:, t * P:(t + 1) * P],
                                                out_scaled[:, l, :], start=True, stop=True)
                    last.then_inc(s_y, 1)

            def entry(u, k):
                l = layer(u)
                e = EXPERTS[l]
                if k == 3:
                    wait_me("E", u)
                    turn_parts("e", u, ME)
                elif k == 4:
                    pe.wait_ge(s_z["e"], u + 1)
                    if u in (0, GROUPS):
                        pe.wait_ge(s_small[l], 16 * 3)
                    for t in range(TILES):
                        z = tok_z[:, u % 2, t * P:(t + 1) * P].bitcast(fp32)
                        last = nc.tensor.matmul(ME[:, t * e:(t + 1) * e], z, gate_raw[:, l, 0:e], start=True, stop=True)
                    last.then_inc(s_lg, 1)
                elif k == 8:
                    pe.wait_ge(s_gates, u + 1)
                    for t in range(TILES):
                        last = turn(ME[0:e, t * P:(t + 1) * P], gates[:, t, 0:e])
                    last.then_inc(s_gateturn, 1)

            def leave(u, k):
                if k == 0:
                    pe.wait_ge(s_sum, adds_before(u + 1))
                    wait_me("X", u)
                    for t in range(TILES):
                        last = turn(ME[:, t * P:(t + 1) * P], total[:, u % 2, t * P:(t + 1) * P])
                    last.then_inc(s_xturn, 1)

            def wait_first(n):
                if n < N0:
                    pe.wait_ge(s_silu_h, n + 1)
                else:
                    pe.wait_ge(s_hid1a, n + 1 - N0)

            def up(u, i):
                n = steps_before(u) + i
                a = 2 * (n % 2)
                if i == 0:
                    pe.wait_ge(s_z["e"], u + 1)
                if i % 2 == 0 and u in (0, GROUPS):
                    pe.wait_ge(s_split, 8 * layer(u) + i // 2 + 1)
                hi, lo = (up_hi1, up_lo1) if layer(u) else (up_hi0, up_lo0)
                z = tok_z[:, u % 2, :]
                if n >= 2:
                    wait_first(n - 2)
                product(UP[:, a, :], hi[:, i, 0, :], lo[:, i, 0, :], z).then_inc(s_upa, 1)
                if n >= 2:
                    wait_hidden(pe, n - 2)
                product(UP[:, a + 1, :], hi[:, i, 1, :], lo[:, i, 1, :], z).then_inc(s_upb, 1)

            def down(u, i):
                q = pairs_before(u) + i
                wait_hidden(pe, 2 * q + 1)
                if q:
                    pe.wait_ge(s_pm, q)
                else:
                    pe.wait_ge(s_biases, 1)
                if i == 0 and u in (0, GROUPS):
                    pe.wait_ge(s_down[layer(u)], 16)
                chunks = 1 + layer(u)
                for j in range(chunks):
                    for k in range(2):
                        w = down1[:, 2 * i + k, j, :] if layer(u) else down0[:, 2 * i + k, :]
                        last = nc.tensor.matmul(DOWN[k * D:(k + 1) * D, :], w, hidden[:, (2 * q + k) % 4, j, :],
                                                start=(j == 0), stop=(j == chunks - 1))
                last.then_inc(s_dn, 1)

            def stages(slot):
                for part, u, k in slot:
                    if part == "A":
                        scans(u, k)
                    elif part == "B":
                        conv(u, k)
                    elif part == "E":
                        entry(u, k)
                    else:
                        leave(u, k)

            pe.wait_ge(s_const, 1)
            def down_due_pair(u, i):
                if i % 2:
                    if i >= LAG:
                        down(u, (i - LAG) // 2)
                    elif u:
                        down(u - 1, PAIRS[layer(u - 1)] - 1)

            for j, slot in enumerate(before):
                if j == 3:
                    pe.wait_ge(s_const, 1)
                    turn_vectors(0, 3, 1)
                elif j == 5:
                    turn_vectors(3, 5, 2)
                elif j == BIASES_AT:
                    small_products()
                stages(slot)
            for u in range(UNITS):
                for i, slot in each_slot(u):
                    if layer(u) == 0:
                        up(u, i)
                        stages(slot)
                        down_due_pair(u, i)
                    else:
                        up(u, i)
                        down_due_pair(u, i)
                        stages(slot)
            down(UNITS - 1, PAIRS[1] - 1)
            leave(UNITS - 1, 0)


_INS = ['x', 'L0_conv_in_w', 'L0_conv_in_b', 'L0_conv_out_w', 'L0_conv_out_b', 'L0_conv_gamma', 'L0_conv_beta',
        'L0_ffn_gate_w', 'L0_ffn_gate_b', 'L0_ffn_w1', 'L0_ffn_w2', 'L0_ffn_w3',
        'L1_conv_in_w', 'L1_conv_in_b', 'L1_conv_out_w', 'L1_conv_out_b', 'L1_conv_gamma', 'L1_conv_beta',
        'L1_ffn_Wg', 'L1_ffn_bg', 'L1_ffn_W1', 'L1_ffn_b1', 'L1_ffn_W2', 'L1_ffn_b2']


def kernel(**inputs):
    import numpy as _np
    import concourse.bacc as _bacc
    from concourse import mybir as _mybir
    from concourse.bass_utils import run_bass_kernel_spmd as _run

    nc = _bacc.Bacc("TRN2", target_bir_lowering=False, num_devices=1)
    arrays, args = {}, []
    for name in _INS:
        a = _np.ascontiguousarray(inputs[name])
        arrays[f"in_{name}_dram"] = a
        args.append(nc.dram_tensor(f"in_{name}_dram", a.shape, _mybir.dt.from_np(a.dtype), kind="ExternalInput").ap())
    args.append(nc.dram_tensor("out_dram", (H, W, B, D), _mybir.dt.float32, kind="ExternalOutput").ap())
    metaformer(nc, *args)
    r = _run(nc, [arrays], core_ids=[0])
    return r.results[0]["out_dram"]
```
